# Optimizing a Trainium2 kernel written in Bass

```python
import numpy as np
import jax
import jax.numpy as jnp

def _softmax(x, axis=-1):
    return jax.nn.softmax(x, axis=axis)

def _gelu(x):
    return jax.nn.gelu(x, approximate=True)

def _silu(x):
    return jax.nn.silu(x)

def _sigmoid(x):
    return jax.nn.sigmoid(x)

def _layernorm(x, axis=-1, eps=1e-05):
    m = jnp.mean(x, axis=axis, keepdims=True)
    v = jnp.var(x, axis=axis, keepdims=True)
    return (x - m) / jnp.sqrt(v + eps)

def _scatter_add(tgt, idx, src, axis=0):
    return tgt.at[idx].add(src)

def _segment_sum(src, seg, n):
    return jax.ops.segment_sum(src, seg, n)
kernel_name = 'mk_gnn_preln_d2_gnn_r16_287ee0'

def setup_inputs(seed: int=0):
    np.random.seed(seed)
    _w = jnp.asarray

    def _rec_inputs():
        import jax
        import jax.numpy as jnp
        _gk = jax.random.key(seed)
        x = -0.0003713 + 1 * jax.random.normal(jax.random.fold_in(_gk, 1), (6250, 128), jnp.float32)
        _s = jax.random.randint(jax.random.fold_in(_gk, 2), (100000,), 0, 6250, jnp.int32)
        _d = jax.random.randint(jax.random.fold_in(_gk, 3), (100000,), 0, 6250, jnp.int32)
        _loop = jnp.arange(6250, dtype=jnp.int32)
        src = jnp.concatenate([_s, _d, _loop])
        dst = jnp.concatenate([_d, _s, _loop])
        _o = jnp.argsort(dst, stable=True)
        src = src[_o]
        dst = dst[_o]
        edge_type_64 = jax.random.randint(jax.random.fold_in(_gk, 13), (206250,), 0, 64, jnp.int32)
        return (x, src, dst, edge_type_64)
    x, src, dst, edge_type_64 = _rec_inputs()

    def _L0_gnn_setup():
        import jax, jax.numpy as jnp
        import numpy as np
        N, E = (6250, 100000)
        NFEAT, NHID, HEADS = (128, 128, 2)
        FOUT = NHID // 2
        NEG_SLOPE = 0.2
        LN_EPS = 1e-05
        key = jax.random.key(seed)
        ks = jax.random.split(key, 10)
        h = jax.random.normal(ks[0], (N, NFEAT), dtype=jnp.float32)
        src = jax.random.randint(ks[1], (E,), 0, N, dtype=jnp.int32)
        dst = jax.random.randint(ks[2], (E,), 0, N, dtype=jnp.int32)
        W = jax.random.normal(ks[3], (NFEAT, HEADS * FOUT), dtype=jnp.float32) / np.sqrt(NFEAT)
        attn_l = jax.random.normal(ks[4], (HEADS, FOUT), dtype=jnp.float32) * 0.1
        attn_r = jax.random.normal(ks[5], (HEADS, FOUT), dtype=jnp.float32) * 0.1
        bias = jnp.zeros((HEADS * FOUT,), dtype=jnp.float32)
        gamma = jnp.ones((NHID,), dtype=jnp.float32)
        beta = jnp.zeros((NHID,), dtype=jnp.float32)
        return {'h': h, 'src': src, 'dst': dst, 'W': W, 'attn_l': attn_l, 'attn_r': attn_r, 'bias': bias, 'gamma': gamma, 'beta': beta}
    _L0_gnn_all = _L0_gnn_setup()
    _L0_gnn_in = {k: v for k, v in _L0_gnn_all.items() if k in ('W', 'attn_l', 'attn_r', 'bias', 'gamma', 'beta')}
    del _L0_gnn_all

    def _L1_gnn_setup():
        import jax, jax.numpy as jnp
        import numpy as np
        N_HOPS = 3
        N_ENTITIES = 6250
        EMB = 128
        N_EDGES = 37500
        N_REL = 64
        key = jax.random.key(seed)
        k1, k2, k3, k4, k5, k6 = jax.random.split(key, 6)
        entity_emb = jax.random.normal(k1, (N_ENTITIES, EMB), dtype=jnp.float32)
        edge_emb = jax.random.normal(k2, (N_REL, EMB), dtype=jnp.float32)
        q_w = jax.random.normal(k3, (EMB, EMB), dtype=jnp.float32) * (1.0 / np.sqrt(EMB))
        k_w = jax.random.normal(k4, (EMB, EMB), dtype=jnp.float32) * (1.0 / np.sqrt(EMB))
        edge_index = jax.random.randint(k5, (2, N_EDGES), 0, N_ENTITIES, dtype=jnp.int64)
        edge_type = jax.random.randint(k6, (N_EDGES,), 0, N_REL, dtype=jnp.int64)
        return {'entity_emb': entity_emb, 'edge_emb': edge_emb, 'q_w': q_w, 'k_w': k_w, 'edge_index': edge_index, 'edge_type': edge_type, 'mess_dropout': 0}
    _L1_gnn_all = _L1_gnn_setup()
    _L1_gnn_in = {k: v for k, v in _L1_gnn_all.items() if k in ('edge_emb', 'q_w', 'k_w')}
    del _L1_gnn_all
    return {'x': x, 'src': src, 'dst': dst, 'edge_type_64': edge_type_64, 'L0_gnn_W': _L0_gnn_in['W'], 'L0_gnn_attn_l': _L0_gnn_in['attn_l'], 'L0_gnn_attn_r': _L0_gnn_in['attn_r'], 'L0_gnn_bias': _L0_gnn_in['bias'], 'L0_gnn_gamma': _L0_gnn_in['gamma'], 'L0_gnn_beta': _L0_gnn_in['beta'], 'L1_gnn_edge_emb': _L1_gnn_in['edge_emb'], 'L1_gnn_q_w': _L1_gnn_in['q_w'], 'L1_gnn_k_w': _L1_gnn_in['k_w']}

def reference(x, src, dst, edge_type_64, L0_gnn_W, L0_gnn_attn_l, L0_gnn_attn_r, L0_gnn_bias, L0_gnn_gamma, L0_gnn_beta, L1_gnn_edge_emb, L1_gnn_q_w, L1_gnn_k_w):
    import jax
    import jax.numpy as jnp

    def _L0_gnn_ref(h, src, dst, W, attn_l, attn_r, bias, gamma, beta):
        import jax, jax.numpy as jnp
        import numpy as np
        N, E = (6250, 100000)
        NFEAT, NHID, HEADS = (128, 128, 2)
        FOUT = NHID // 2
        NEG_SLOPE = 0.2
        LN_EPS = 1e-05
        feat = (h @ W).reshape(N, HEADS, FOUT)
        el = jnp.einsum('nhf,hf->nh', feat, attn_l)
        er = jnp.einsum('nhf,hf->nh', feat, attn_r)
        e = jax.nn.leaky_relu(el[src] + er[dst], NEG_SLOPE)
        emax = jax.ops.segment_max(e, dst, num_segments=N)
        expe = jnp.exp(e - emax[dst])
        denom = jax.ops.segment_sum(expe, dst, num_segments=N)
        alpha = expe / denom[dst]
        msg = feat[src] * alpha[:, :, None]
        out = jax.ops.segment_sum(msg, dst, num_segments=N)
        x = out.reshape(N, HEADS * FOUT) + bias
        mu = jnp.mean(x, axis=-1, keepdims=True)
        var = jnp.mean(jnp.square(x - mu), axis=-1, keepdims=True)
        return gamma * (x - mu) * jax.lax.rsqrt(var + LN_EPS) + beta

    def _L1_gnn_ref(entity_emb, edge_emb, q_w, k_w, edge_index, edge_type, mess_dropout):
        import jax, jax.numpy as jnp
        import numpy as np
        N_HOPS = 3
        N_ENTITIES = 6250
        EMB = 128
        N_EDGES = 37500
        N_REL = 64
        head = edge_index[0]
        tail = edge_index[1]
        rel = edge_emb[edge_type]
        n = entity_emb.shape[0]
        agg = entity_emb
        out = jnp.zeros_like(entity_emb)
        for _ in range(N_HOPS):
            h = agg[head]
            t = agg[tail]
            left = h @ q_w
            right = jnp.tanh(rel * t @ k_w)
            att = jnp.sum(left * right, axis=1)
            seg_max = jax.ops.segment_max(att, head, num_segments=n)
            e = jnp.exp(att - seg_max[head])
            seg_sum = jax.ops.segment_sum(e, head, num_segments=n)
            w = e / seg_sum[head]
            msg = w[:, None] * rel * t
            summed = jax.ops.segment_sum(msg, head, num_segments=n)
            cnt = jax.ops.segment_sum(jnp.ones_like(att), head, num_segments=n)
            agg = summed / jnp.maximum(cnt, 1.0)[:, None]
            norm = jnp.linalg.norm(agg, axis=1, keepdims=True)
            agg = agg / jnp.maximum(norm, 1e-12)
            out = out + agg + entity_emb
        return out
    edge_index = jnp.stack([src, dst])
    h = jnp.maximum(_layernorm(x, axis=-1), 0.0)
    x = x + _L0_gnn_ref(h, src, dst, L0_gnn_W, L0_gnn_attn_l, L0_gnn_attn_r, L0_gnn_bias, L0_gnn_gamma, L0_gnn_beta)
    h = jnp.maximum(_layernorm(x, axis=-1), 0.0)
    x = x + _L1_gnn_ref(h, L1_gnn_edge_emb, L1_gnn_q_w, L1_gnn_k_w, edge_index, edge_type_64, 0)
    return x

_drawn_inputs = setup_inputs


def setup_inputs(seed=0):
    import zlib

    import numpy as np

    out = dict(_drawn_inputs(seed))
    spreads = {'L0_gnn_bias': (0.0, 0.1), 'L0_gnn_gamma': (1.0, 0.2), 'L0_gnn_beta': (0.0, 0.1)}
    factors = {}
    for name, (base, spread) in spreads.items():
        noise = np.random.default_rng([zlib.crc32(name.encode()), seed]).standard_normal(out[name].shape)
        drawn = base * np.exp(spread * noise) if base else spread * noise
        out[name] = jnp.asarray(drawn.astype(out[name].dtype))
    for name, factor in factors.items():
        out[name] = (out[name] * factor).astype(out[name].dtype)
    return out
```

```python
from contextlib import ExitStack

import concourse.bass as bass
import concourse.mybir as mybir

P = 128
N = 6250
E = 206250
F = 128
NB = -(-N // P)
NLAST = N - (NB - 1) * P
HEADS = 2
FH = F // HEADS
RELS = 64
HOPS = 3
SLOPE = 0.2
EPS = 1e-5

G = 256
U = 14
R = 7
BODIES = -(-((E - NB) // G + NB) // U)
NG = BODIES * U
COLS = -(-E // P)
LASTCOLS = E - (P - 1) * COLS
CH = 31
CHUNKS = COLS // (2 * CH)
ROWS = P * COLS + G
SHIFT = 13
MASK = (1 << SHIFT) - 1
NOWHERE = 400000.0
BIG = 1e30
ARENA = 20800
FB = -(-NB // 3)
LB = -(-NB // 4)
SW = F + 2
TW = 2 * (FH + 2)
MW = 6
KEEP, RESET, NKEEP, FORGET, TARGET = range(5)
assert 2 * CH * CHUNKS == COLS and N < MASK and RELS <= 64 and E * 64 + NB < 1 << 24

ALU = mybir.AluOpType
ACT = mybir.ActivationFunctionType
AX = mybir.AxisListType.X
F32 = mybir.dt.float32
BF16 = mybir.dt.bfloat16
I32 = mybir.dt.int32
U16 = mybir.dt.uint16


class Body:

    def __init__(self, eng, hop, i, uses):
        self.first = isinstance(i, int) and i == 0
        self.last = isinstance(i, int) and i == BODIES
        self.at = i * U if isinstance(i, int) else eng.snap(i * U)
        self.eng = eng

        def value(per_hop, per_body):
            v = i * per_body
            if hop is not None:
                v = v + hop * per_hop
            return v if isinstance(v, int) else eng.snap(v)

        self.groups = value(NG, U)
        self.used = {name: value(BODIES * (U // ring) * inc, (U // ring) * inc) for name, (ring, inc) in uses.items()}
        self.uses = uses

    def has(self, j):
        return (j >= 0 or not self.first) and (j < 0 or not self.last)

    def count(self, j):
        return self.groups + (j + 1)

    def landed(self, name, j):
        ring, inc = self.uses[name]
        return self.used[name] + inc * (j // ring + 1)


def pipeline(eng, hop, step, uses):
    b = Body(eng, hop, 0, uses)
    for k in range(U):
        step(b, k)
    with eng.Fori(1, BODIES) as i:
        b = Body(eng, hop, i, uses)
        for k in range(U):
            step(b, k)
    b = Body(eng, hop, BODIES, uses)
    for k in range(U):
        step(b, k)


def gnn_kernel(nc, x, src, dst, etype, w, attn_l, attn_r, bias, gamma, beta, emb, q_w, k_w, out):
    with ExitStack() as ctx:
        ctx.enter_context(nc.allow_non_contiguous_dma(reason="narrow columns of edges and scores"))

        def sb(name, shape, dt=F32):
            return ctx.enter_context(nc.sbuf_tensor(name, shape, dt))

        def sem(name):
            return ctx.enter_context(nc.semaphore(name))

        def dram(name, shape, dt):
            return nc.dram_tensor(name, shape, dt).ap()

        sorted_edges = [dram(f"sorted_edges{s}", (ROWS, 1), I32) for s in range(2)]
        key_d = [dram(f"key{s}_d", (ROWS,), U16) for s in range(2)]
        peer_d = [dram(f"peer{s}_d", (ROWS,), I32) for s in range(2)]
        type_d = dram("type_d", (ROWS,), U16)
        meta_d = [dram(f"meta{s}_d", (P, NG, MW), F32) for s in range(2)]
        feat_d = dram("feat_d", (NB * P, TW), F32)
        er_d = dram("er_d", (NB, P, HEADS), F32)
        agg_d = dram("agg_d", (NB * P, F), F32)
        left_d = dram("left_d", (NB, F, P), F32)
        state_d = dram("state_d", (NG, P, SW), F32)

        xs = sb("xs", [P, NB, F])
        agg = sb("agg", [P, NB, F])
        tmp = sb("tmp", [P, NB, F])
        wide = sb("wide", [P, NB * TW])
        state = wide[:, 0:NB * SW].rearrange("p (b c) -> p b c", c=SW)
        feat = wide[:, 0:NB * TW].rearrange("p (b c) -> p b c", c=TW)
        left = wide[:, 0:NB * P].rearrange("p (b c) -> p b c", c=P)
        er = sb("er", [P, NB, HEADS])
        stat = [sb(f"stat{i}", [P, NB, 2]) for i in range(3)]

        ident = sb("ident", [P, P])
        ones = sb("ones", [P, P])
        before = sb("before", [P, P])
        upto = sb("upto", [P, P])
        rowid = sb("rowid", [P, P])
        giota = sb("giota", [P, NG])
        biota = sb("biota", [P, 64])
        w_s = sb("w_s", [P, F])
        wx = sb("wx", [P, TW + HEADS])
        junk = sb("junk", [P, FH])
        al_s = sb("al_s", [P, F])
        ar_s = sb("ar_s", [P, F])
        bias_s = sb("bias_s", [P, F])
        gamma_s = sb("gamma_s", [P, F])
        beta_s = sb("beta_s", [P, F])
        emb_s = sb("emb_s", [RELS, F])
        emb_rest = sb("emb_rest", [RELS, F])
        emb3 = sb("emb3", [RELS, 3, F], BF16)
        qw_s = sb("qw_s", [P, F])
        kw_s = sb("kw_s", [P, F])
        plan = [sb(f"plan{s}", [P, NG], I32) for s in range(2)]
        lastg = [sb(f"lastg{s}", [P, NB], I32) for s in range(2)]
        few = sb("few", [P, 16])
        fewi = sb("fewi", [P, 2], I32)
        counts = sb("counts", [P, NB])
        rows = [sb(f"rows{i}", [P, NB]) for i in range(4)]
        rowsi = sb("rowsi", [P, NB], I32)
        stage = sb("stage", [P, 2, 2, CH], I32)
        colid = sb("colid", [P, P])
        few_wide = sb("few_wide", [P, P])
        rowsi2 = sb("rowsi2", [P, NB], I32)
        sent_u = sb("sent_u", [P, G // P], U16)
        zero_u = sb("zero_u", [P, G // P], U16)
        zero_i = sb("zero_i", [P, G // P], I32)
        tmp_flat = tmp[:].rearrange("p b f -> p (b f)")
        tmp_meta = tmp_flat[:, 0:NG * MW]
        agg_flat = agg[:].rearrange("p b f -> p (b f)")
        scratch = [agg_flat[:, i * NG:(i + 1) * NG] for i in range(4)]
        member = agg_flat[:, 4 * NG:5 * NG]
        valT_r = tmp_flat[:, 1024:1024 + R * G].rearrange("p (a b) -> p a b", a=R)
        right_r = tmp_flat[:, 1024 + R * G:1024 + 2 * R * G].rearrange("p (a b) -> p a b", a=R)
        batchT = tmp_flat[:, 0:1024].rearrange("p (a b) -> p a b", a=2)

        arena = sb("arena", [P, ARENA])

        def column(i, dt=F32):
            a = arena[:, i * COLS:(i + 1) * COLS]
            return a if dt is F32 else a.bitcast(dt)[:, 0:COLS]

        src_i, dst_i, type_i = column(0, I32), column(1, I32), column(2, I32)
        pos_f, run_f = column(3), column(4)
        pos_i = [column(5, I32), column(6, I32)]
        packed, spare_i = column(7, I32), column(8, I32)
        high = column(9, BF16)
        mask = column(10, U16)
        half = column(11, U16)
        ring_at = [0]

        def ring(shape, dt=F32):
            n = 1
            for d in shape:
                n *= d
            words = n if dt in (F32, I32) else -(-n // 2)
            a = arena[:, ring_at[0]:ring_at[0] + words]
            ring_at[0] += words
            assert ring_at[0] <= ARENA
            if dt is not F32:
                a = a.bitcast(dt)
            if len(shape) == 2:
                return a.rearrange("p (a b) -> p a b", a=shape[0])
            return a.rearrange("p (a b c) -> p a b c", a=shape[0], b=shape[1])

        peer_r = ring((R, 2), I32)
        key_r = ring((R, G), U16)
        type_r = ring((R, G), U16)
        meta_r = ring((U, MW))
        er_r = ring((R, HEADS))
        left_r = ring((U, P))
        rows_r = ring((R, 2, TW))
        hot_r = ring((R, G), BF16)
        off_r = ring((R, G), BF16)
        val_r = ring((R, 2, F + 1))
        nohit_r = ring((R, G), BF16)
        cnt_r = ring((R, 1))
        min_in_r = ring((R, HEADS))
        fade_r = ring((R, HEADS))
        min_r = ring((R, HEADS))
        alpha_r = ring((R, HEADS))
        acc_r = ring((R, SW))
        relu_r = ring((2, HEADS * G))
        score_r = ring((R, HEADS * G))
        prob_r = ring((2, HEADS * G))
        probT_r = ring((R, 2 * HEADS, P))

        bank = [ctx.enter_context(nc.psum_tensor(f"bank{i}", [P, 512], F32)) for i in range(8)]

        inputs_in = sem("inputs_in")
        edges_in = sem("edges_in")
        pads_set = sem("pads_set")
        consts_made = sem("consts_made")
        rowid_made = sem("rowid_made")
        dve_step = sem("dve_step")
        bucket_step = sem("bucket_step")
        count_step = sem("count_step")
        hop_step = sem("hop_step")
        counts_ready = sem("counts_ready")
        totals_ready = sem("totals_ready")
        groups_ready = sem("groups_ready")
        ends_ready = sem("ends_ready")
        member_ready = sem("member_ready")
        blocks_ready = sem("blocks_ready")
        positions_ready = sem("positions_ready")
        meta_ready = sem("meta_ready")
        meta_stored = sem("meta_stored")
        staged = [sem(f"staged{i}") for i in range(2)]
        scattered = [sem(f"scattered{i}") for i in range(2)]
        resorted_in = sem("resorted_in")
        decoded = sem("decoded")
        sorted_stored = sem("sorted_stored")
        sentinel_set = sem("sentinel_set")
        var_ready = sem("var_ready")
        std_ready = sem("std_ready")
        hidden_ready = sem("hidden_ready")
        hiddenT_ready = sem("hiddenT_ready")
        hiddenT_copied = sem("hiddenT_copied")
        feat_ready = sem("feat_ready")
        feat_copied = sem("feat_copied")
        feat_whole = sem("feat_whole")
        feat_stored = sem("feat_stored")
        weights_ready = sem("weights_ready")
        agg_ready = sem("agg_ready")
        aggT_ready = sem("aggT_ready")
        aggT_copied = sem("aggT_copied")
        left_ready = sem("left_ready")
        left_copied = sem("left_copied")
        hop_stored = sem("hop_stored")
        state_in = sem("state_in")
        hop_done = sem("hop_done")
        out_ready = sem("out_ready")
        out_stored = sem("out_stored")
        passed = {e.engine: sem(f"passed{i}") for i, e in enumerate((nc.vector, nc.gpsimd, nc.sync))}
        pipes = []
        for q in ("attn_", "hop_"):
            pipes.append({
                "loaded": [sem(f"{q}loaded{i}") for i in range(U)],
                "gathered": [sem(f"{q}gathered{i}") for i in range(R)],
                "stored": [sem(f"{q}stored{i}") for i in range(R)],
                **{n: sem(q + n) for n in (
                    "off_done", "min_in_done", "scores_ready", "relu_done", "neg_done", "min_done", "exp_done",
                    "probT_ready", "probT_copied", "sum_ready", "acc_done", "rel_ready", "val_done", "valT_ready",
                    "valT_copied", "right_ready", "right_done")},
            })
        block = ctx.enter_context(nc.Block())

        def apart(eng):
            eng.sem_inc(passed[eng.engine], 1)

        def lanes(array, a0=0):
            return array[a0:a0 + P * COLS].rearrange("(p c) -> p c", p=P)

        uses = [{"loaded": (U, 64), "gathered": (R, 32), "stored": (R, 16)},
                {"loaded": (U, 80), "gathered": (R, 32), "stored": (R, 16)}]
        STORE = [10, 13]

        @block.sync
        def _(sp):
            sp.wait_ge(pads_set, 1)
            for a, d in ((src_i, src), (dst_i, dst), (type_i, etype)):
                sp.dma_start(a[0:P - 1, :], d[0:(P - 1) * COLS].rearrange("(p c) -> p c", p=P - 1)).then_inc(edges_in, 16)
                sp.dma_start(a[P - 1:P, 0:LASTCOLS], d[(P - 1) * COLS:E].rearrange("(p c) -> p c", p=1)).then_inc(edges_in, 16)
            sp.dma_start(xs[:, 0:NB - 1, :], x[0:(NB - 1) * P, :].rearrange("(b p) f -> p b f", p=P)).then_inc(inputs_in, 16)
            sp.dma_start(xs[0:NLAST, NB - 1, :], x[(NB - 1) * P:N, :]).then_inc(inputs_in, 16)
            for a, d in ((w_s, w), (qw_s, q_w), (kw_s, k_w), (emb_s, emb)):
                sp.dma_start(a[:], d).then_inc(inputs_in, 16)
            for a, d in ((al_s, attn_l.rearrange("a b -> (a b)")), (ar_s, attn_r.rearrange("a b -> (a b)")), (bias_s, bias), (gamma_s, gamma), (beta_s, beta)):
                sp.dma_start(a[:], d.partition_broadcast(P)).then_inc(inputs_in, 16)

            for s in range(2):
                sp.wait_ge(meta_ready, s + 1)
                sp.dma_start(meta_d[s].rearrange("p g c -> p (g c)"), (wide[:, 0:NG * MW], tmp_meta)[s]).then_inc(meta_stored, 16)
                sp.wait_ge(positions_ready, s + 1)

                def stage_chunk(i, h, first):
                    if not first:
                        sp.wait_ge(scattered[h], sp.snap(i * (16 * CH) + (s * CHUNKS) * 16 * CH))
                        apart(sp)
                    at = i * (2 * CH) + h * CH
                    sp.dma_start(stage[:, h, 0, :], pos_i[s][:, bass.ds(at, CH)]).then_inc(staged[h], 16)
                    sp.dma_start(stage[:, h, 1, :], packed[:, bass.ds(at, CH)]).then_inc(staged[h], 16)

                for h in range(2):
                    stage_chunk(0, h, s == 0)
                with sp.Fori(1, CHUNKS) as i:
                    for h in range(2):
                        stage_chunk(i, h, False)
            for s in range(2):
                if s == 0:
                    for h in range(2):
                        sp.wait_ge(scattered[h], 2 * CHUNKS * 16 * CH)
                sp.wait_ge(sentinel_set, s + 1)
                e = sorted_edges[s].rearrange("e o -> (e o)")
                sp.dma_start(packed[0:P - 1, :], e[0:(P - 1) * COLS].rearrange("(p c) -> p c", p=P - 1)).then_inc(resorted_in, 16)
                sp.dma_start(packed[P - 1:P, 0:LASTCOLS], e[(P - 1) * COLS:E].rearrange("(p c) -> p c", p=1)).then_inc(resorted_in, 16)
                sp.wait_ge(decoded, s + 1)
                sp.dma_start(lanes(key_d[s]), mask).then_inc(sorted_stored, 16)
                sp.dma_start(key_d[s][P * COLS:ROWS].rearrange("(p c) -> p c", p=P), sent_u[:]).then_inc(sorted_stored, 16)
                sp.dma_start(lanes(peer_d[s]), spare_i).then_inc(sorted_stored, 16)
                sp.dma_start(peer_d[s][P * COLS:ROWS].rearrange("(p c) -> p c", p=P), zero_i[:]).then_inc(sorted_stored, 16)
                if s == 1:
                    sp.dma_start(lanes(type_d), half).then_inc(sorted_stored, 16)
                    sp.dma_start(type_d[P * COLS:ROWS].rearrange("(p c) -> p c", p=P), zero_u[:]).then_inc(sorted_stored, 16)
            sp.wait_ge(feat_whole, 1)
            sp.dma_start(feat_d.rearrange("(b p) c -> p b c", p=P), feat).then_inc(feat_stored, 16)
            sp.dma_start(er_d.rearrange("b p h -> p b h"), er[:]).then_inc(feat_stored, 16)
            sp.wait_ge(meta_stored, 32)
            sp.wait_ge(sorted_stored, 10 * 16)
            sp.wait_ge(feat_stored, 32)

            def load_store(layer):
                q = pipes[layer]

                def step(b, k):
                    j = k
                    if not b.last:
                        n = b.groups + k if not b.first else k
                        if not (b.first and k < R):
                            sp.wait_ge(q["gathered"][j % R], b.landed("gathered", j - R))
                            apart(sp)
                            sp.wait_ge(q["off_done"], b.count(j - R))
                            apart(sp)
                            if layer == 0:
                                sp.wait_ge(q["relu_done"], b.count(j - R))
                                apart(sp)
                        if not b.first:
                            sp.wait_ge(q["acc_done"], b.count(j - U))
                        apart(sp)
                        g = k if b.first else b.at + k
                        both = sp.value_load(plan[layer][0:1, g:g + 1] if b.first else plan[layer][0:1, bass.ds(g, 1)],
                                             min_val=0, max_val=E * 64 + 63)
                        e0 = nc.s_assert_within(both >> 6, 0, E)
                        blk = nc.s_assert_within(both & 63, 0, NB - 1)
                        d = q["loaded"][j % U]
                        sp.dma_start(peer_r[:, j % R, :], peer_d[layer][bass.ds(e0, G)].rearrange("(p c) -> p c", p=P)).then_inc(d, 16)
                        sp.dma_start(key_r[:, j % R, :], key_d[layer][bass.ds(e0, G)].partition_broadcast(P)).then_inc(d, 16)
                        sp.dma_start(meta_r[:, j % U, :], meta_d[layer][:, bass.ds(g, 1), :].rearrange("p o c -> p (o c)")).then_inc(d, 16)
                        if layer == 0:
                            sp.dma_start(er_r[:, j % R, :], er_d[bass.ds(blk, 1)].rearrange("o p c -> p (o c)")).then_inc(d, 16)
                        else:
                            sp.dma_start(type_r[0:RELS, j % R, :], type_d[bass.ds(e0, G)].partition_broadcast(RELS)).then_inc(d, 16)
                            sp.dma_start(left_r[:, j % U, :], left_d[bass.ds(blk, 1)].rearrange("o f n -> f (o n)")).then_inc(d, 16)
                    j = k - STORE[layer]
                    if b.has(j):
                        sp.wait_ge(q["acc_done"], b.count(j))
                        apart(sp)
                        g = b.at + j
                        sp.dma_start(state_d[g] if isinstance(g, int) else state_d[bass.ds(g, 1)].rearrange("o p c -> p (o c)"),
                                     acc_r[:, j % R, :]).then_inc(q["stored"][j % R], 16)
                return step

            def load_states(layer):
                apart(sp)
                with sp.Fori(0, NB) as b:
                    g = sp.value_load(lastg[layer][0:1, bass.ds(b, 1)], min_val=0, max_val=NG - 1)
                    sp.dma_start(wide[:, bass.ds(b * SW, SW)], state_d[bass.ds(g, 1)].rearrange("o p c -> p (o c)")).then_inc(state_in, 16)

            pipeline(sp, None, load_store(0), uses[0])
            for i in range(R):
                sp.wait_ge(pipes[0]["stored"][i], 16 * (NG // R))
            load_states(0)

            with sp.Fori(0, HOPS) as hop:
                sp.wait_ge(agg_ready, hop + 1)
                sp.dma_start(agg_d.rearrange("(b p) f -> p b f", p=P), agg[:]).then_inc(hop_stored, 16)
                sp.wait_ge(left_copied, sp.snap(hop * LB + LB))
                sp.dma_start(left_d.rearrange("b f n -> f b n"), left).then_inc(hop_stored, 16)
                sp.wait_ge(hop_stored, sp.snap(hop * 32 + 32))
                pipeline(sp, hop, load_store(1), uses[1])
                for i in range(R):
                    sp.wait_ge(pipes[1]["stored"][i], sp.snap(hop * (16 * (NG // R)) + 16 * (NG // R)))
                load_states(1)
                sp.wait_ge(hop_done, hop + 1)
                apart(sp)
            sp.wait_ge(out_ready, 1)
            sp.dma_start(out[0:(NB - 1) * P, :].rearrange("(b p) f -> p b f", p=P), xs[:, 0:NB - 1, :]).then_inc(out_stored, 16)
            sp.dma_start(out[(NB - 1) * P:N, :], xs[0:NLAST, NB - 1, :]).then_inc(out_stored, 16)
            sp.wait_ge(out_stored, 32)

        @block.gpsimd
        def _(pool):
            nc.gpsimd.iota(giota[:], [[1, NG]], base=0, channel_multiplier=0, allow_small_or_imprecise_dtypes=True)
            nc.gpsimd.iota(biota[:], [[1, 64]], base=0, channel_multiplier=0, allow_small_or_imprecise_dtypes=True)
            nc.gpsimd.iota(rowid[:], [[0, P]], base=0, channel_multiplier=1, allow_small_or_imprecise_dtypes=True)
            nc.gpsimd.iota(colid[:], [[1, P]], base=0, channel_multiplier=0, allow_small_or_imprecise_dtypes=True).then_inc(rowid_made, 1)

            for s in range(2):
                with pool.Fori(0, CHUNKS) as i:
                    for h in range(2):
                        pool.wait_ge(staged[h], pool.snap(i * 32 + (s * CHUNKS + 1) * 32))
                        apart(pool)
                        for c in range(CH):
                            nc.gpsimd.indirect_dma_start(
                                out=sorted_edges[s], out_offset=bass.IndirectOffsetOnAxis(ap=stage[:, h, 0, c:c + 1], axis=0),
                                in_=stage[:, h, 1, c:c + 1], in_offset=None, bounds_check=E - 1, oob_is_err=False,
                            ).then_inc(scattered[h], 16)

            def gather(layer):
                q = pipes[layer]
                table = (feat_d, agg_d)[layer]
                width = (TW, F)[layer]

                def step(b, k):
                    if b.last:
                        return
                    pool.wait_ge(q["loaded"][k % U], b.landed("loaded", k))
                    if not (b.first and k < R):
                        pool.wait_ge(q["sum_ready" if layer == 0 else "val_done"], b.count(k - R))
                    apart(pool)
                    for c in range(2):
                        nc.gpsimd.indirect_dma_start(
                            out=rows_r[:, k % R, c, 0:width], out_offset=None, in_=table,
                            in_offset=bass.IndirectOffsetOnAxis(ap=peer_r[:, k % R, c:c + 1], axis=0),
                        ).then_inc(q["gathered"][k % R], 16)
                return step

            pool.wait_ge(feat_stored, 32)
            pipeline(pool, None, gather(0), uses[0])
            with pool.Fori(0, HOPS) as hop:
                pool.wait_ge(hop_stored, pool.snap(hop * 32 + 32))
                apart(pool)
                pipeline(pool, hop, gather(1), uses[1])

        @block.tensor
        def _(pe):
            def mm(out, lhsT, rhs, start=True, stop=True):
                return nc.tensor.matmul(out, lhsT, rhs, start=start, stop=stop)

            pe.wait_ge(consts_made, 1)
            for s in range(2):
                pe.wait_ge(counts_ready, s + 1)
                mm(bank[0][:, 0:NB], before[:], counts[:])
                mm(bank[1][:, 0:NB], ones[:], counts[:])
                mm(bank[2][0:NB, 0:1], counts[:], ones[:, 0:1]).then_inc(totals_ready, 1)
                pe.wait_ge(groups_ready, s + 1)
                mm(bank[3][0:NB, 0:1], before[0:NB, 0:NB], few[0:NB, 0:1])
                mm(bank[4][0:NB, 0:1], upto[0:NB, 0:NB], few[0:NB, 1:2]).then_inc(ends_ready, 1)
                pe.wait_ge(member_ready, s + 1)
                for h in range(2):
                    mm(bank[5 + h][:, 0:NG // 2], rowid[0:NB, :], member[0:NB, h * (NG // 2):(h + 1) * (NG // 2)])
                for h in range(2):
                    last = mm(bank[(7, 0)[h]][:, 0:NG // 2], few_wide[0:NB, :], member[0:NB, h * (NG // 2):(h + 1) * (NG // 2)])
                last.then_inc(blocks_ready, 1)

            pe.wait_ge(hidden_ready, 1)
            pe.wait_ge(weights_ready, 1)
            for t in range(FB + 1):
                if t < FB:
                    if t >= 2:
                        pe.wait_ge(hiddenT_copied, t - 1)
                    for i in range(min(3, NB - 3 * t)):
                        last = nc.tensor.transpose(bank[t % 2][:, i * P:(i + 1) * P], agg[:, 3 * t + i, :], ident[:])
                    last.then_inc(hiddenT_ready, 1)
                if t >= 1:
                    pe.wait_ge(hiddenT_copied, t)
                    if t >= 3:
                        pe.wait_ge(feat_copied, t - 2)
                    for i in range(min(3, NB - 3 * (t - 1))):
                        last = mm(bank[2 + (t - 1) % 2][:, i * (TW + HEADS):(i + 1) * (TW + HEADS)],
                                  batchT[:, (t - 1) % 2, i * P:(i + 1) * P], wx[:])
                    last.then_inc(feat_ready, 1)

            q = pipes[0]

            def attn_step(b, k):
                j = k - 5
                if b.has(j):
                    pe.wait_ge(q["gathered"][j % R], b.landed("gathered", j))
                    if not (b.first and j < 2):
                        pe.wait_ge(q["neg_done"], b.count(j - 2))
                    elif b.first and j == 0:
                        pe.wait_ge(feat_whole, 1)
                    for h in range(HEADS):
                        for c in range(2):
                            last = nc.tensor.transpose(
                                bank[j % 2][:, h * G + c * P:h * G + (c + 1) * P],
                                rows_r[:, j % R, c, h * (FH + 2) + FH + 1:h * (FH + 2) + FH + 2].to_broadcast([P, P]), ident[:])
                    last.then_inc(q["scores_ready"], 1)
                j = k - 7
                if b.has(j):
                    pe.wait_ge(q["exp_done"], b.count(j))
                    for i in range(2 * HEADS):
                        last = nc.tensor.transpose(bank[2 + j % 2][:, i * P:(i + 1) * P], prob_r[:, j % 2, i * P:(i + 1) * P], ident[:])
                    last.then_inc(q["probT_ready"], 1)
                j = k - 8
                if b.has(j):
                    if not (b.first and j < 2):
                        pe.wait_ge(q["acc_done"], b.count(j - 2))
                    pe.wait_ge(q["probT_copied"], b.count(j))
                    for h in range(HEADS):
                        for c in range(2):
                            last = mm(bank[4 + j % 2][:, h * (FH + 1):(h + 1) * (FH + 1)], probT_r[:, j % R, 2 * h + c, :],
                                      rows_r[:, j % R, c, h * (FH + 2):h * (FH + 2) + FH + 1], c == 0, c == 1)
                    last.then_inc(q["sum_ready"], 1)

            pipeline(pe, None, attn_step, uses[0])

            h_ = pipes[1]

            def hop_pe_step(b, k):
                q = h_
                j = k - 11
                if b.has(j):
                    if not (b.first and j < 2):
                        pe.wait_ge(q["acc_done"], b.count(j - 2))
                    pe.wait_ge(q["probT_copied"], b.count(j))
                    for c in range(2):
                        last = mm(bank[5 + j % 2][:, 0:F + 1], probT_r[:, j % R, c, :], val_r[:, j % R, c, :], c == 0, c == 1)
                    last.then_inc(q["sum_ready"], 1)
                j = k - 10
                if b.has(j):
                    pe.wait_ge(q["exp_done"], b.count(j))
                    for c in range(2):
                        last = nc.tensor.transpose(bank[4][:, c * P:(c + 1) * P], prob_r[:, j % 2, c * P:(c + 1) * P], ident[:])
                    last.then_inc(q["probT_ready"], 1)
                j = k - 8
                if b.has(j):
                    pe.wait_ge(q["right_done"], b.count(j))
                    mm(bank[(3, 7)[j % 2]][:, 0:G], left_r[:, j % U, :], right_r[:, j % R, :]).then_inc(q["scores_ready"], 1)
                j = k - 7
                if b.has(j):
                    pe.wait_ge(q["valT_copied"], b.count(j))
                    mm(bank[2][:, 0:G], kw_s[:], valT_r[:, j % R, :]).then_inc(q["right_ready"], 1)
                j = k - 6
                if b.has(j):
                    pe.wait_ge(q["val_done"], b.count(j))
                    for c in range(2):
                        last = nc.tensor.transpose(bank[1][:, c * P:(c + 1) * P], val_r[:, j % R, c, 0:F], ident[:])
                    last.then_inc(q["valT_ready"], 1)
                j = k - 5
                if b.has(j):
                    pe.wait_ge(q["off_done"], b.count(j))
                    for c in range(2):
                        for i in range(3):
                            last = mm(bank[0][:, c * P:(c + 1) * P], hot_r[0:RELS, j % R, c * P:(c + 1) * P], emb3[:, i, :], i == 0, i == 2)
                    last.then_inc(q["rel_ready"], 1)

            with pe.Fori(0, HOPS) as hop:
                pe.wait_ge(agg_ready, hop + 1)
                tiles = pe.snap(hop * LB)
                for t in range(LB + 1):
                    if t < LB:
                        if t >= 2:
                            pe.wait_ge(aggT_copied, tiles + (t - 1))
                        for i in range(min(4, NB - 4 * t)):
                            last = nc.tensor.transpose(bank[t % 2][:, i * P:(i + 1) * P], agg[:, 4 * t + i, :], ident[:])
                        last.then_inc(aggT_ready, 1)
                    if t >= 1:
                        pe.wait_ge(aggT_copied, tiles + t)
                        if t >= 3:
                            pe.wait_ge(left_copied, tiles + (t - 2))
                        n = min(4, NB - 4 * (t - 1)) * P
                        mm(bank[2 + (t - 1) % 2][:, 0:n], qw_s[:], batchT[:, (t - 1) % 2, 0:n]).then_inc(left_ready, 1)
                pe.wait_ge(left_copied, tiles + LB)
                pipeline(pe, hop, hop_pe_step, uses[1])

        @block.scalar
        def _(act):
            def root(n):
                act.wait_ge(var_ready, n)
                nc.scalar.activation(stat[2][:, :, 0:1], stat[1][:, :, 0:1], ACT.Sqrt).then_inc(std_ready, 1)

            root(1)
            for t in range(FB):
                act.wait_ge(hiddenT_ready, t + 1)
                if t >= 2:
                    act.wait_ge(feat_ready, t - 1)
                n = min(3, NB - 3 * t) * P
                nc.scalar.copy(batchT[:, t % 2, 0:n], bank[t % 2][:, 0:n]).then_inc(hiddenT_copied, 1)
            q = pipes[0]

            def attn_step(b, k):
                j = k - 7
                if b.has(j):
                    act.wait_ge(q["min_done"], b.count(j))
                    for h in range(HEADS):
                        nc.scalar.activation(alpha_r[:, j % R, h:h + 1], min_r[:, j % R, h:h + 1], ACT.Exp, bias=fade_r[:, j % R, h:h + 1])
                    for h in range(HEADS):
                        last = nc.scalar.activation(prob_r[:, j % 2, h * G:(h + 1) * G], score_r[:, j % R, h * G:(h + 1) * G],
                                                    ACT.Exp, scale=-1.0, bias=min_r[:, j % R, h:h + 1])
                    last.then_inc(q["exp_done"], 1)
                j = k - 5
                if b.has(j):
                    act.wait_ge(q["scores_ready"], b.count(j))
                    for h in range(HEADS):
                        last = nc.scalar.activation(relu_r[:, j % 2, h * G:(h + 1) * G], bank[j % 2][:, h * G:(h + 1) * G],
                                                    ACT.Relu, scale=1.0 - SLOPE, bias=er_r[:, j % R, h:h + 1])
                    last.then_inc(q["relu_done"], 1)
                j = k - 7
                if b.has(j):
                    act.wait_ge(q["probT_ready"], b.count(j))
                    nc.scalar.copy(probT_r[:, j % R, :, :], bank[2 + j % 2][:].rearrange("p (a b) -> p a b", b=P)).then_inc(q["probT_copied"], 1)

            pipeline(act, None, attn_step, uses[0])
            root(2)
            root(3)
            h_ = pipes[1]

            def hop_act_step(b, k):
                q = h_
                j = k - 9
                if b.has(j):
                    act.wait_ge(q["min_done"], b.count(j))
                    nc.scalar.activation(prob_r[:, j % 2, 0:G], score_r[:, j % R, 0:G], ACT.Exp, scale=-1.0,
                                         bias=min_r[:, j % R, 0:1]).then_inc(q["exp_done"], 1)
                    nc.scalar.activation(alpha_r[:, j % R, 0:1], min_r[:, j % R, 0:1], ACT.Exp, bias=fade_r[:, j % R, 0:1])
                    nc.scalar.activation(nohit_r[:, j % R, :], off_r[:, j % R, :], ACT.Exp, scale=-1.0, accum_out=cnt_r[:, j % R, 0:1])
                j = k - 10
                if b.has(j):
                    act.wait_ge(q["probT_ready"], b.count(j))
                    nc.scalar.copy(probT_r[:, j % R, 0:2, :], bank[4][:, 0:G].rearrange("p (a b) -> p a b", b=P)).then_inc(q["probT_copied"], 1)
                j = k - 7
                if b.has(j):
                    act.wait_ge(q["right_ready"], b.count(j))
                    nc.scalar.activation(right_r[:, j % R, :], bank[2][:, 0:G], ACT.Tanh).then_inc(q["right_done"], 1)
                j = k - 6
                if b.has(j):
                    act.wait_ge(q["valT_ready"], b.count(j))
                    nc.scalar.copy(valT_r[:, j % R, :], bank[1][:, 0:G]).then_inc(q["valT_copied"], 1)

            with act.Fori(0, HOPS) as hop:
                tiles = act.snap(hop * LB)
                for t in range(LB):
                    act.wait_ge(aggT_ready, tiles + (t + 1))
                    if t >= 2:
                        act.wait_ge(left_ready, tiles + (t - 1))
                    n = min(4, NB - 4 * t) * P
                    nc.scalar.copy(batchT[:, t % 2, 0:n], bank[t % 2][:, 0:n]).then_inc(aggT_copied, 1)
                pipeline(act, hop, hop_act_step, uses[1])
                act.wait_ge(var_ready, hop + 4)
                nc.scalar.activation(stat[2][:, :, 0:1], stat[1][:, :, 0:1], ACT.Sqrt).then_inc(std_ready, 1)

        @block.vector
        def _(dve):
            V = nc.vector
            steps = [0]

            def do(ins):
                ins.then_inc(dve_step, 1)
                steps[0] += 1
                dve.wait_ge(dve_step, steps[0])

            def signal(s):
                dve.sem_inc(s, 1)

            for a in (src_i, dst_i, type_i):
                V.memset(a, MASK)
            V.memset(xs[:], 0.0)
            V.memset(wx[:], 0.0).then_inc(pads_set, 1)
            V.memset(ones[:], 1.0)
            V.memset(sent_u[:], MASK)
            V.memset(zero_u[:], 0)
            do(V.memset(zero_i[:], 0))
            dve.wait_ge(rowid_made, 1)
            V.tensor_tensor(ident[:], rowid[:], colid[:], ALU.is_equal)
            V.tensor_tensor(before[:], rowid[:], colid[:], ALU.is_lt)
            V.tensor_tensor(upto[:], rowid[:], colid[:], ALU.is_le).then_inc(consts_made, 1)
            dve.wait_ge(edges_in, 6 * 16)

            def find_positions(s):
                key = (dst_i, src_i)[s]
                if s == 1:
                    for h in range(2):
                        dve.wait_ge(scattered[h], CHUNKS * 16 * CH)
                do(V.tensor_scalar(spare_i, key, 7, None, ALU.logical_shift_right))
                do(V.tensor_copy(high, spare_i))
                with dve.Fori(0, NB) as b:
                    n = dve.snap(b + s * NB)
                    dve.wait_ge(count_step, n)
                    V.tensor_scalar(mask.bitcast(BF16), high, biota[:, bass.ds(b, 1)], None, ALU.is_equal, ALU.add,
                                    accum_out=counts[:, bass.ds(b, 1)]).then_inc(count_step, 1)
                dve.wait_ge(count_step, (s + 1) * NB)
                signal(counts_ready)
                dve.wait_ge(totals_ready, s + 1)
                do(V.tensor_copy(few[0:NB, 0:1], bank[2][0:NB, 0:1]))
                do(V.tensor_scalar(few[0:NB, 2:3], few[0:NB, 0:1], float(G - 1), None, ALU.add))
                do(V.tensor_copy(fewi[0:NB, 0:1], few[0:NB, 2:3]))
                do(V.tensor_scalar(fewi[0:NB, 1:2], fewi[0:NB, 0:1], G.bit_length() - 1, None, ALU.logical_shift_right))
                do(V.tensor_copy(few[0:NB, 3:4], fewi[0:NB, 1:2]))
                do(V.tensor_scalar(few[0:NB, 1:2], few[0:NB, 3:4], 1.0, None, ALU.max))
                signal(groups_ready)
                do(V.tensor_scalar(rows[0][:], bank[1][:, 0:NB], float(G - 1), None, ALU.add))
                do(V.tensor_copy(rowsi[:], rows[0][:]))
                do(V.tensor_scalar(rowsi2[:], rowsi[:], G.bit_length() - 1, None, ALU.logical_shift_right))
                do(V.tensor_copy(rows[0][:], rowsi2[:]))
                do(V.tensor_scalar(rows[1][:], rows[0][:], 1.0, None, ALU.max))
                do(V.tensor_tensor_scan(rows[2][:], ones[:, 0:NB], rows[1][:], 0.0, ALU.mult, ALU.add))
                do(V.tensor_scalar(lastg[s][:], rows[2][:], -1.0, None, ALU.add))
                do(V.tensor_copy(rows[0][:], bank[1][:, 0:NB]))
                do(V.tensor_tensor_scan(rows[1][:], ones[:, 0:NB], rows[0][:], 0.0, ALU.mult, ALU.add))
                do(V.tensor_tensor(rows[2][:], rows[1][:], rows[0][:], ALU.subtract))
                do(V.tensor_tensor(rows[3][:], rows[2][:], bank[0][:, 0:NB], ALU.add))
                dve.wait_ge(ends_ready, s + 1)
                do(V.tensor_copy(few[0:NB, 4:5], bank[4][0:NB, 0:1]))
                do(V.tensor_tensor(few[0:NB, 5:6], few[0:NB, 4:5], few[0:NB, 1:2], ALU.subtract))
                do(V.scalar_tensor_tensor(few[0:NB, 6:7], few[0:NB, 5:6], -float(G), bank[3][0:NB, 0:1], ALU.mult, ALU.add))
                do(V.tensor_scalar(few[0:NB, 7:8], rowid[0:NB, 0:1], float(NB - 1), 1e6, ALU.is_equal, ALU.mult))
                do(V.tensor_tensor(few[0:NB, 8:9], few[0:NB, 7:8], few[0:NB, 4:5], ALU.add))
                do(V.tensor_scalar(few_wide[0:NB, :], ones[0:NB, :], few[0:NB, 6:7], None, ALU.mult))
                do(V.tensor_scalar(scratch[0][0:NB, :], giota[0:NB, :], few[0:NB, 5:6], None, ALU.is_ge))
                do(V.scalar_tensor_tensor(member[0:NB, :], giota[0:NB, :], few[0:NB, 8:9], scratch[0][0:NB, :], ALU.is_lt, ALU.mult))
                signal(member_ready)
                dve.wait_ge(blocks_ready, s + 1)
                half_g = NG // 2
                for h in range(2):
                    do(V.tensor_copy(scratch[1][:, h * half_g:(h + 1) * half_g], bank[5 + h][:, 0:half_g]))
                    do(V.scalar_tensor_tensor(scratch[2][:, h * half_g:(h + 1) * half_g], giota[:, h * half_g:(h + 1) * half_g],
                                              float(G), bank[(7, 0)[h]][:, 0:half_g], ALU.mult, ALU.add))
                do(V.tensor_scalar(scratch[2], scratch[2], float(E), 64.0, ALU.min, ALU.mult))
                do(V.tensor_tensor(scratch[3], scratch[2], scratch[1], ALU.add))
                do(V.tensor_copy(plan[s][:], scratch[3]))
                meta = (wide[:, 0:NG * MW], tmp_meta)[s].rearrange("p (g c) -> p g c", c=MW)
                m = [meta[:, :, i] for i in range(MW)]
                do(V.memset(meta, 0.0))
                do(V.tensor_tensor(m[KEEP][:, 1:NG], scratch[1][:, 1:NG], scratch[1][:, 0:NG - 1], ALU.is_equal))
                do(V.tensor_scalar(m[RESET], m[KEEP], -0.5 * BIG, 0.5 * BIG, ALU.mult, ALU.add))
                do(V.tensor_scalar(m[NKEEP], m[KEEP], -1.0, None, ALU.mult))
                do(V.tensor_scalar(m[FORGET], m[KEEP], 0.75 * BIG, -0.75 * BIG, ALU.mult, ALU.add))
                do(V.tensor_scalar(m[TARGET], scratch[1], float(P), rowid[:, 0:1], ALU.mult, ALU.add))
                signal(meta_ready)
                do(V.memset(pos_f, NOWHERE))
                with dve.Fori(0, NB) as b:
                    n = dve.snap(b * 3 + s * 3 * NB)
                    dve.wait_ge(bucket_step, n)
                    V.tensor_scalar(mask, high, biota[:, bass.ds(b, 1)], None, ALU.is_equal).then_inc(bucket_step, 1)
                    dve.wait_ge(bucket_step, n + 1)
                    V.tensor_tensor_scan(run_f, ones[:, 0:1].to_broadcast([P, COLS]), mask, rows[3][:, bass.ds(b, 1)], ALU.mult, ALU.add).then_inc(bucket_step, 1)
                    dve.wait_ge(bucket_step, n + 2)
                    apart(dve)
                    V.copy_predicated(pos_f, mask, run_f).then_inc(bucket_step, 1)
                dve.wait_ge(bucket_step, (s + 1) * 3 * NB)
                do(V.tensor_scalar(pos_i[s], pos_f, -1.0, None, ALU.add))
                if s == 0:
                    do(V.tensor_scalar(spare_i, type_i, 2 * SHIFT, None, ALU.logical_shift_left))
                    do(V.tensor_scalar(packed, dst_i, SHIFT, None, ALU.logical_shift_left))
                    do(V.tensor_tensor(spare_i, spare_i, packed, ALU.bitwise_or))
                    do(V.tensor_tensor(packed, spare_i, src_i, ALU.bitwise_or))
                signal(positions_ready)

            find_positions(0)
            find_positions(1)

            def norm(src_t, dst_t, n):
                do(V.reduce_sum(stat[0][:, :, 0], src_t, axis=AX))
                do(V.tensor_scalar(stat[0][:, :, 1], stat[0][:, :, 0], 1.0 / F, None, ALU.mult))
                do(V.tensor_tensor(tmp[:], src_t, stat[0][:, :, 1:2].to_broadcast([P, NB, F]), ALU.subtract))
                do(V.tensor_tensor(dst_t, tmp[:], tmp[:], ALU.mult))
                do(V.reduce_sum(stat[1][:, :, 1], dst_t, axis=AX))
                do(V.tensor_scalar(stat[1][:, :, 0], stat[1][:, :, 1], 1.0 / F, EPS, ALU.mult, ALU.add))
                signal(var_ready)
                dve.wait_ge(std_ready, n)
                do(V.reciprocal(stat[2][:, :, 1], stat[2][:, :, 0]))
                do(V.tensor_tensor(dst_t, tmp[:], stat[2][:, :, 1:2].to_broadcast([P, NB, F]), ALU.mult))

            dve.wait_ge(inputs_in, 11 * 16)
            for h in range(HEADS):
                c0 = h * (FH + 2)
                do(V.tensor_copy(wx[:, c0:c0 + FH], w_s[:, h * FH:(h + 1) * FH]))
                do(V.tensor_tensor(junk[:], w_s[:, h * FH:(h + 1) * FH], al_s[:, h * FH:(h + 1) * FH], ALU.mult))
                do(V.reduce_sum(wx[:, c0 + FH + 1:c0 + FH + 2], junk[:], axis=AX))
                do(V.tensor_tensor(junk[:], w_s[:, h * FH:(h + 1) * FH], ar_s[:, h * FH:(h + 1) * FH], ALU.mult))
                do(V.reduce_sum(wx[:, TW + h:TW + h + 1], junk[:], axis=AX))
            do(V.tensor_copy(emb3[:, 0, :], emb_s[:]))
            do(V.tensor_tensor(emb_rest[:], emb_s[:], emb3[:, 0, :], ALU.subtract))
            do(V.tensor_copy(emb3[:, 1, :], emb_rest[:]))
            do(V.tensor_tensor(emb_s[:], emb_rest[:], emb3[:, 1, :], ALU.subtract))
            do(V.tensor_copy(emb3[:, 2, :], emb_s[:]))
            signal(weights_ready)

            dve.wait_ge(meta_stored, 32)
            norm(xs[:], agg[:], 1)
            do(V.tensor_scalar(agg[:], agg[:], 0.0, None, ALU.max))
            signal(hidden_ready)
            for t in range(FB):
                dve.wait_ge(feat_ready, t + 1)
                k = min(3, NB - 3 * t)
                s_ = bank[2 + t % 2][:, 0:k * (TW + HEADS)].rearrange("p (b c) -> p b c", b=k)
                V.tensor_copy(feat[:, 3 * t:3 * t + k, :], s_[:, :, 0:TW])
                V.tensor_scalar(er[:, 3 * t:3 * t + k, :], s_[:, :, TW:TW + HEADS], 1.0 - SLOPE, None, ALU.mult).then_inc(feat_copied, 1)
            dve.wait_ge(feat_copied, FB)
            for h in range(HEADS):
                do(V.memset(feat[:, :, h * (FH + 2) + FH:h * (FH + 2) + FH + 1], 1.0))
            signal(feat_whole)

            for s in range(2):
                if s == 0:
                    for h in range(2):
                        dve.wait_ge(scattered[h], 2 * CHUNKS * 16 * CH)
                else:
                    dve.wait_ge(sorted_stored, 4 * 16)
                do(V.memset(packed, (MASK << SHIFT, MASK)[s]))
                signal(sentinel_set)
                dve.wait_ge(resorted_in, (s + 1) * 32)
                do(V.tensor_scalar(src_i, packed, MASK, None, ALU.bitwise_and))
                do(V.tensor_scalar(dst_i, packed, SHIFT, MASK, ALU.logical_shift_right, ALU.bitwise_and))
                do(V.tensor_scalar(type_i, packed, 2 * SHIFT, None, ALU.logical_shift_right))
                do(V.tensor_copy(mask, (dst_i, src_i)[s]))
                do(V.tensor_copy(spare_i, (src_i, dst_i)[s]))
                do(V.tensor_copy(half, type_i))
                signal(decoded)
            dve.wait_ge(sorted_stored, 10 * 16)
            do(V.memset(acc_r, 0.0))
            do(V.memset(min_r, 0.0))
            dve.wait_ge(feat_stored, 32)

            def state_columns(layer):
                if layer == 0:
                    return acc_r[:, :, 0:HEADS * (FH + 1)]
                return acc_r

            q0 = pipes[0]

            def masks(q, b, j, layer):
                dve.wait_ge(q["loaded"][j % U], b.landed("loaded", j))
                if layer == 1:
                    V.tensor_scalar(hot_r[0:RELS, j % R, :].rearrange("n (c p) -> n c p", c=2),
                                    type_r[0:RELS, j % R, :].rearrange("n (p c) -> n c p", c=2), rowid[0:RELS, 0:1], None, ALU.is_equal)
                V.tensor_scalar(off_r[:, j % R, :].rearrange("n (c p) -> n c p", c=2),
                                key_r[:, j % R, :].rearrange("n (p c) -> n c p", c=2),
                                meta_r[:, j % U, TARGET:TARGET + 1], BIG, ALU.not_equal, ALU.mult).then_inc(q["off_done"], 1)

            def start_min(q, b, j, n):
                m = meta_r[:, j % U, :]
                if not (b.first and j == 0):
                    dve.wait_ge(q["min_done"], b.count(j - 1))
                V.tensor_scalar(min_in_r[:, j % R, 0:n], min_r[:, (j - 1) % R, 0:n], m[:, KEEP:KEEP + 1], m[:, RESET:RESET + 1], ALU.mult, ALU.add)
                V.tensor_scalar(fade_r[:, j % R, 0:n], min_r[:, (j - 1) % R, 0:n], m[:, NKEEP:NKEEP + 1], m[:, FORGET:FORGET + 1],
                                ALU.mult, ALU.add).then_inc(q["min_in_done"], 1)

            def accumulate(q, b, j):
                dve.wait_ge(q["sum_ready"], b.count(j))
                if not (b.first and j == 0):
                    dve.wait_ge(q["acc_done"], b.count(j - 1))
                if not (b.first and j < R):
                    dve.wait_ge(q["stored"][j % R], b.landed("stored", j - R))

            def attn_step(b, k):
                q = q0
                j = k - 9
                if b.has(j):
                    accumulate(q, b, j)
                    for h in range(HEADS):
                        c = slice(h * (FH + 1), (h + 1) * (FH + 1))
                        last = V.scalar_tensor_tensor(acc_r[:, j % R, c], acc_r[:, (j - 1) % R, c], alpha_r[:, j % R, h:h + 1],
                                                      bank[4 + j % 2][:, c], ALU.mult, ALU.add)
                    last.then_inc(q["acc_done"], 1)
                j = k - 6
                if b.has(j):
                    start_min(q, b, j, HEADS)
                    dve.wait_ge(q["relu_done"], b.count(j))
                    V.scalar_tensor_tensor(score_r[:, j % R, :], bank[j % 2][:], -SLOPE, relu_r[:, j % 2, :], ALU.mult, ALU.subtract).then_inc(q["neg_done"], 1)
                j = k - 4
                if b.has(j):
                    masks(q, b, j, 0)
                j = k - 6
                if b.has(j):
                    dve.wait_ge(q["min_in_done"], b.count(j))
                    dve.wait_ge(q["neg_done"], b.count(j))
                    apart(dve)
                    for h in range(HEADS):
                        last = V.tensor_tensor_reduce(out=score_r[:, j % R, h * G:(h + 1) * G], in0=score_r[:, j % R, h * G:(h + 1) * G],
                                                      in1=off_r[:, j % R, :], scale=1.0, scalar=min_in_r[:, j % R, h:h + 1],
                                                      op0=ALU.add, op1=ALU.min, accum_out=min_r[:, j % R, h:h + 1])
                    last.then_inc(q["min_done"], 1)

            pipeline(dve, None, attn_step, uses[0])

            dve.wait_ge(state_in, NB * 16)
            st = state.rearrange("p b (h c) -> p b h c", h=HEADS)
            do(V.tensor_scalar(stat[0][:], st[:, :, :, FH], 1e-30, None, ALU.max))
            do(V.reciprocal(stat[1][:], stat[0][:]))
            for h in range(HEADS):
                do(V.tensor_tensor(agg[:, :, h * FH:(h + 1) * FH], st[:, :, h, 0:FH], stat[1][:, :, h:h + 1].to_broadcast([P, NB, FH]), ALU.mult))
            every = lambda a: a[:].rearrange("p (o f) -> p o f", o=1).to_broadcast([P, NB, F])
            do(V.tensor_tensor(agg[:], agg[:], every(bias_s), ALU.add))
            norm(agg[:], agg[:], 2)
            do(V.tensor_tensor(agg[:], agg[:], every(gamma_s), ALU.mult))
            do(V.tensor_tensor(agg[:], agg[:], every(beta_s), ALU.add))
            do(V.tensor_tensor(xs[:], xs[:], agg[:], ALU.add))
            norm(xs[:], agg[:], 3)
            do(V.tensor_scalar(agg[:], agg[:], 0.0, None, ALU.max))
            do(V.scalar_tensor_tensor(xs[:], agg[:], float(HOPS), xs[:], ALU.mult, ALU.add))
            do(V.memset(val_r, 1.0))
            do(V.memset(acc_r, 0.0))
            signal(agg_ready)
            q1 = pipes[1]

            def hop_dve_step(b, k):
                q = q1
                j = k - 12
                if b.has(j):
                    accumulate(q, b, j)
                    V.tensor_scalar(acc_r[:, j % R, F + 1:F + 2], acc_r[:, (j - 1) % R, F + 1:F + 2], meta_r[:, j % U, KEEP:KEEP + 1],
                                    cnt_r[:, j % R, 0:1], ALU.mult, ALU.add)
                    V.scalar_tensor_tensor(acc_r[:, j % R, 0:F + 1], acc_r[:, (j - 1) % R, 0:F + 1], alpha_r[:, j % R, 0:1],
                                           bank[5 + j % 2][:, 0:F + 1], ALU.mult, ALU.add).then_inc(q["acc_done"], 1)
                j = k - 8
                if b.has(j):
                    start_min(q, b, j, 1)
                j = k - 4
                if b.has(j):
                    masks(q, b, j, 1)
                j = k - 8
                if b.has(j):
                    dve.wait_ge(q["min_in_done"], b.count(j))
                    dve.wait_ge(q["scores_ready"], b.count(j))
                    apart(dve)
                    V.tensor_tensor_reduce(out=score_r[:, j % R, 0:G], in0=bank[(3, 7)[j % 2]][:, 0:G], in1=off_r[:, j % R, :],
                                           scale=1.0, scalar=min_in_r[:, j % R, 0:1], op0=ALU.add, op1=ALU.min,
                                           accum_out=min_r[:, j % R, 0:1]).then_inc(q["min_done"], 1)
                j = k - 5
                if b.has(j):
                    dve.wait_ge(q["gathered"][j % R], b.landed("gathered", j))
                    dve.wait_ge(q["rel_ready"], b.count(j))
                    V.tensor_tensor(val_r[:, j % R, :, 0:F], rows_r[:, j % R, :, 0:F],
                                    bank[0][:, 0:G].rearrange("p (c f) -> p c f", c=2), ALU.mult).then_inc(q["val_done"], 1)

            HOP_STEPS = 13
            with dve.Fori(0, HOPS) as hop:
                at = dve.snap(hop * HOP_STEPS)
                n = [0]

                def hdo(ins):
                    ins.then_inc(hop_step, 1)
                    n[0] += 1
                    dve.wait_ge(hop_step, at + n[0])

                tiles = dve.snap(hop * LB)
                for t in range(LB):
                    dve.wait_ge(left_ready, tiles + (t + 1))
                    k = min(4, NB - 4 * t)
                    V.tensor_scalar(wide[:, 4 * t * P:(4 * t + k) * P], bank[2 + t % 2][:, 0:k * P], -1.0, None, ALU.mult).then_inc(left_copied, 1)
                pipeline(dve, hop, hop_dve_step, uses[1])
                dve.wait_ge(state_in, dve.snap(hop * (NB * 16) + 2 * NB * 16))
                hdo(V.tensor_scalar(stat[0][:, :, 0:1], state[:, :, F:F + 1], 1e-30, None, ALU.max))
                hdo(V.tensor_scalar(stat[0][:, :, 1:2], state[:, :, F + 1:F + 2], 1.0, None, ALU.max))
                hdo(V.reciprocal(stat[1][:], stat[0][:]))
                hdo(V.tensor_tensor(stat[2][:, :, 0:1], stat[1][:, :, 0:1], stat[1][:, :, 1:2], ALU.mult))
                hdo(V.tensor_tensor(agg[:], state[:, :, 0:F], stat[2][:, :, 0:1].to_broadcast([P, NB, F]), ALU.mult))
                hdo(V.tensor_tensor(tmp[:], agg[:], agg[:], ALU.mult))
                hdo(V.reduce_sum(stat[0][:, :, 0], tmp[:], axis=AX))
                hdo(V.tensor_scalar(stat[1][:, :, 0:1], stat[0][:, :, 0:1], 1e-24, None, ALU.max))
                dve.sem_inc(var_ready, 1)
                dve.wait_ge(std_ready, hop + 4)
                hdo(V.reciprocal(stat[2][:, :, 1], stat[2][:, :, 0]))
                hdo(V.tensor_tensor(agg[:], agg[:], stat[2][:, :, 1:2].to_broadcast([P, NB, F]), ALU.mult))
                hdo(V.tensor_tensor(xs[:], xs[:], agg[:], ALU.add))
                hdo(V.memset(acc_r, 0.0))
                hdo(V.memset(min_r, 0.0))
                assert n[0] == HOP_STEPS
                dve.sem_inc(hop_done, 1)
                dve.sem_inc(agg_ready, 1)
            dve.sem_inc(out_ready, 1)


_INS = ["x", "src", "dst", "edge_type_64", "L0_gnn_W", "L0_gnn_attn_l", "L0_gnn_attn_r", "L0_gnn_bias", "L0_gnn_gamma",
        "L0_gnn_beta", "L1_gnn_edge_emb", "L1_gnn_q_w", "L1_gnn_k_w"]


def kernel(**inputs):
    import numpy as np
    import concourse.bacc as bacc
    from concourse.bass_utils import run_bass_kernel_spmd

    nc = bacc.Bacc("TRN2", target_bir_lowering=False, num_devices=1)
    arrays, args = {}, []
    for name in _INS:
        a = np.ascontiguousarray(inputs[name])
        arrays[f"in_{name}"] = a
        args.append(nc.dram_tensor(f"in_{name}", a.shape, mybir.dt.from_np(a.dtype), kind="ExternalInput").ap())
    result = nc.dram_tensor("out_x", (N, F), F32, kind="ExternalOutput").ap()
    gnn_kernel(nc, *args, result)
    r = run_bass_kernel_spmd(nc, [arrays], core_ids=[0])
    return r.results[0]["out_x"]
```

```python
from contextlib import ExitStack

import concourse.bass as bass
import concourse.mybir as mybir

P = 128
N = 6250
E = 206250
F = 128
NB = -(-N // P)
NLAST = N - (NB - 1) * P
HEADS = 2
FH = F // HEADS
RELS = 64
HOPS = 3
SLOPE = 0.2
EPS = 1e-5

G = 256
U = 14
R = 7
BODIES = -(-((E - NB) // G + NB) // U)
NG = BODIES * U
COLS = -(-E // P)
LASTCOLS = E - (P - 1) * COLS
CH = 31
CHUNKS = COLS // (2 * CH)
TILES = NG * G // P
LANES = TILES // U
WIDTH = U * P
SHIFT = 13
PADKEY = 7 << 10
MASK = (1 << SHIFT) - 1
NOWHERE = 400000.0
BIG = 1e30
ARENA = 10 * COLS
FB = -(-NB // 3)
LB = -(-NB // 4)
SW = F + 2
TW = 2 * (FH + 2)
MW = 6
KEEP, RESET, NKEEP, FORGET, TARGET = range(5)
assert 2 * CH * CHUNKS == COLS and N < MASK and RELS <= 64 and E * 64 + NB < 1 << 24

ALU = mybir.AluOpType
ACT = mybir.ActivationFunctionType
AX = mybir.AxisListType.X
F32 = mybir.dt.float32
BF16 = mybir.dt.bfloat16
I32 = mybir.dt.int32
U16 = mybir.dt.uint16


class Body:

    def __init__(self, eng, hop, i, uses):
        self.first = isinstance(i, int) and i == 0
        self.last = isinstance(i, int) and i == BODIES
        self.at = i * U if isinstance(i, int) else eng.snap(i * U)
        self.eng = eng

        def value(per_hop, per_body):
            v = i * per_body
            if hop is not None:
                v = v + hop * per_hop
            return v if isinstance(v, int) else eng.snap(v)

        self.groups = value(NG, U)
        self.used = {name: value(BODIES * (U // ring) * inc, (U // ring) * inc) for name, (ring, inc) in uses.items()}
        self.uses = uses

    def has(self, j):
        return (j >= 0 or not self.first) and (j < 0 or not self.last)

    def count(self, j):
        return self.groups + (j + 1)

    def landed(self, name, j):
        ring, inc = self.uses[name]
        return self.used[name] + inc * (j // ring + 1)


def pipeline(eng, hop, step, uses):
    b = Body(eng, hop, 0, uses)
    for k in range(U):
        step(b, k)
    with eng.Fori(1, BODIES) as i:
        b = Body(eng, hop, i, uses)
        for k in range(U):
            step(b, k)
    b = Body(eng, hop, BODIES, uses)
    for k in range(U):
        step(b, k)


def gnn_kernel(nc, x, src, dst, etype, w, attn_l, attn_r, bias, gamma, beta, emb, q_w, k_w, out):
    with ExitStack() as ctx:
        ctx.enter_context(nc.allow_non_contiguous_dma(reason="narrow columns of edges and scores"))

        def sb(name, shape, dt=F32):
            return ctx.enter_context(nc.sbuf_tensor(name, shape, dt))

        def sem(name):
            return ctx.enter_context(nc.semaphore(name))

        def dram(name, shape, dt):
            return nc.dram_tensor(name, shape, dt).ap()

        sorted_edges = [dram(f"sorted_edges{s}", (NG * G, 1), I32) for s in range(2)]
        key_d = [dram(f"key{s}_d", (NG * G,), U16) for s in range(2)]
        type_d = dram("type_d", (NG * G,), U16)
        meta_d = [dram(f"meta{s}_d", (P, NG, MW), F32) for s in range(2)]
        feat_d = dram("feat_d", (NB * P, TW), F32)
        er_d = dram("er_d", (NB, P, HEADS), F32)
        agg_d = dram("agg_d", (NB * P, F), F32)
        left_d = dram("left_d", (NB, F, P), F32)
        state_d = dram("state_d", (P, NG * SW), F32)

        xs = sb("xs", [P, NB, F])
        agg = sb("agg", [P, NB, F])
        tmp = sb("tmp", [P, NB, F])
        wide = sb("wide", [P, NB * TW])
        state = wide[:, 0:NB * SW].rearrange("p (b c) -> p b c", c=SW)
        feat = wide[:, 0:NB * TW].rearrange("p (b c) -> p b c", c=TW)
        left = wide[:, 0:NB * P].rearrange("p (b c) -> p b c", c=P)
        er = sb("er", [P, NB, HEADS])
        stat = [sb(f"stat{i}", [P, NB, 2]) for i in range(3)]

        ident = sb("ident", [P, P])
        ones = sb("ones", [P, P])
        before = sb("before", [P, P])
        upto = sb("upto", [P, P])
        rowid = sb("rowid", [P, P])
        giota = sb("giota", [P, NG])
        biota = sb("biota", [P, 64])
        w_s = sb("w_s", [P, F])
        wx = sb("wx", [P, TW + HEADS])
        junk = sb("junk", [P, FH])
        al_s = sb("al_s", [P, F])
        ar_s = sb("ar_s", [P, F])
        bias_s = sb("bias_s", [P, F])
        gamma_s = sb("gamma_s", [P, F])
        beta_s = sb("beta_s", [P, F])
        emb_s = sb("emb_s", [RELS, F])
        emb_rest = sb("emb_rest", [RELS, F])
        emb3 = sb("emb3", [RELS, 3, F], BF16)
        qw_s = sb("qw_s", [P, F])
        kw_s = sb("kw_s", [P, F])
        plan = [sb(f"plan{s}", [P, NG], I32) for s in range(2)]
        peers = [sb(f"peers{s}", [P, TILES], I32) for s in range(2)]
        lastg = [sb(f"lastg{s}", [P, NB], I32) for s in range(2)]
        few = sb("few", [P, 16])
        fewi = sb("fewi", [P, 2], I32)
        counts = sb("counts", [P, NB])
        rows = [sb(f"rows{i}", [P, NB]) for i in range(4)]
        rowsi = sb("rowsi", [P, NB], I32)
        stage = sb("stage", [P, 2, 2, CH], I32)
        colid = sb("colid", [P, P])
        rowsi2 = sb("rowsi2", [P, NB], I32)
        tmp_flat = tmp[:].rearrange("p b f -> p (b f)")
        tmp_meta = tmp_flat[:, 0:NG * MW]
        agg_flat = agg[:].rearrange("p b f -> p (b f)")
        scratch = [agg_flat[:, i * NG:(i + 1) * NG] for i in range(4)]
        member = agg_flat[:, 4 * NG:5 * NG]
        batchT = tmp_flat[:, 0:1024].rearrange("p (a b) -> p a b", a=2)

        arena = sb("arena", [P, ARENA])

        def column(i, dt=F32, cols=COLS, n=P, odd=0):
            a = arena[:, i * cols:(i + 1) * cols]
            return (a if dt is F32 else a.bitcast(dt))[0:n, odd * cols:(odd + 1) * cols]

        src_i, dst_i, type_i = column(0, I32), column(1, I32), column(2, I32)
        pos_f, run_f = column(3), column(4)
        pos_i = [column(5, I32), column(6, I32)]
        packed, spare_i = column(7, I32), column(8, I32)
        high = column(9, BF16)
        mask = column(9, U16, odd=1)
        s_packed, s_src, s_dst, s_type, s_part = (column(i, I32, WIDTH, LANES) for i in (0, 1, 2, 3, 4))
        s_peer = column(5, F32, WIDTH, LANES)
        s_key, s_type16 = column(6, U16, WIDTH, LANES), column(7, U16, WIDTH, LANES)
        sentinel = wide[0:LANES, 0:WIDTH].bitcast(I32)
        spaces = {"arena": [arena[:], 0, ARENA], "agg": [agg_flat, 0, NB * F], "tmp": [tmp_flat, 1024, NB * F], "wide": [wide[:], 0, NB * TW]}

        def ring(shape, dt=F32, space="arena"):
            n = 1
            for d in shape:
                n *= d
            words = n if dt in (F32, I32) else -(-n // 2)
            flat, at, end = spaces[space]
            a = flat[:, at:at + words]
            spaces[space][1] += words
            assert at + words <= end, space
            if dt is not F32:
                a = a.bitcast(dt)
            if len(shape) == 2:
                return a.rearrange("p (a b) -> p a b", a=shape[0])
            return a.rearrange("p (a b c) -> p a b c", a=shape[0], b=shape[1])

        peer_r = ring((U, 2), I32)
        key_r = ring((U, G), U16, "wide")
        type_r = ring((U, G), U16, "wide")
        unit_meta = ring((U, MW))
        meta_r = ring((U, MW))
        er_r = ring((U, HEADS))
        left_r = ring((U, P), F32, "wide")
        rows_r = ring((R, 2, TW), F32, "agg")
        hot_r = ring((R, G), BF16)
        off_r = ring((R, G), BF16)
        val_r = ring((R, 2, F + 1))
        nohit_r = ring((R, G), BF16, "tmp")
        valT_r = ring((R, G), F32, "tmp")
        right_r = ring((R, G), F32, "tmp")
        cnt_r = ring((R, 1))
        min_in_r = ring((R, HEADS))
        fade_r = ring((R, HEADS))
        min_r = ring((R, HEADS))
        alpha_r = ring((R, HEADS))
        acc_r = ring((U, SW))
        relu_r = ring((2, HEADS * G))
        score_r = ring((R, HEADS * G), F32, "agg")
        prob_r = ring((2, HEADS * G))
        probT_r = ring((R, 2 * HEADS, P))

        bank = [ctx.enter_context(nc.psum_tensor(f"bank{i}", [P, 512], F32)) for i in range(8)]

        inputs_in = sem("inputs_in")
        edges_in = sem("edges_in")
        pads_set = sem("pads_set")
        consts_made = sem("consts_made")
        rowid_made = sem("rowid_made")
        dve_step = sem("dve_step")
        bucket_step = sem("bucket_step")
        count_step = sem("count_step")
        hop_step = sem("hop_step")
        counts_ready = sem("counts_ready")
        totals_ready = sem("totals_ready")
        groups_ready = sem("groups_ready")
        ends_ready = sem("ends_ready")
        member_ready = sem("member_ready")
        blocks_ready = sem("blocks_ready")
        positions_ready = sem("positions_ready")
        meta_ready = sem("meta_ready")
        meta_stored = sem("meta_stored")
        staged = [sem(f"staged{i}") for i in range(2)]
        scattered = [sem(f"scattered{i}") for i in range(2)]
        resorted_in = sem("resorted_in")
        decoded = sem("decoded")
        sorted_stored = sem("sorted_stored")
        peerT_ready = sem("peerT_ready")
        peerT_copied = sem("peerT_copied")
        prefilled = sem("prefilled")
        var_ready = sem("var_ready")
        std_ready = sem("std_ready")
        hidden_ready = sem("hidden_ready")
        hiddenT_ready = sem("hiddenT_ready")
        hiddenT_copied = sem("hiddenT_copied")
        feat_ready = sem("feat_ready")
        feat_copied = sem("feat_copied")
        feat_whole = sem("feat_whole")
        feat_stored = sem("feat_stored")
        weights_ready = sem("weights_ready")
        agg_ready = sem("agg_ready")
        aggT_ready = sem("aggT_ready")
        aggT_copied = sem("aggT_copied")
        left_ready = sem("left_ready")
        left_copied = sem("left_copied")
        hop_stored = sem("hop_stored")
        state_in = sem("state_in")
        hop_done = sem("hop_done")
        out_ready = sem("out_ready")
        out_stored = sem("out_stored")
        passed = {e.engine: sem(f"passed{i}") for i, e in enumerate((nc.vector, nc.gpsimd, nc.sync))}
        pipes_free = sem("pipes_free")
        pipes = []
        for q in ("attn_", "hop_"):
            pipes.append({
                "unit": [sem(f"{q}unit_loaded{i}") for i in range(2)],
                "block": [sem(f"{q}block_loaded{i}") for i in range(U)],
                "gathered": [sem(f"{q}gathered{i}") for i in range(R)],
                "stored": [sem(f"{q}stored{i}") for i in range(2)],
                **{n: sem(q + n) for n in (
                    "off_done", "min_in_done", "scores_ready", "relu_done", "neg_done", "min_done", "exp_done",
                    "probT_ready", "probT_copied", "sum_ready", "acc_done", "rel_ready", "val_done", "valT_ready",
                    "valT_copied", "right_ready", "right_done")},
            })
        block = ctx.enter_context(nc.Block())

        def apart(eng):
            eng.sem_inc(passed[eng.engine], 1)

        uses = [{"unit": (U, 48), "block": (U, 16), "gathered": (R, 32), "stored": (U, 16)},
                {"unit": (U, 64), "block": (U, 16), "gathered": (R, 32), "stored": (U, 16)}]
        STORE = [10, 13]

        @block.sync
        def _(sp):
            sp.wait_ge(pads_set, 1)
            for a, d in ((src_i, src), (dst_i, dst), (type_i, etype)):
                sp.dma_start(a[0:P - 1, :], d[0:(P - 1) * COLS].rearrange("(p c) -> p c", p=P - 1)).then_inc(edges_in, 16)
                sp.dma_start(a[P - 1:P, 0:LASTCOLS], d[(P - 1) * COLS:E].rearrange("(p c) -> p c", p=1)).then_inc(edges_in, 16)
            for s in range(2):
                sp.dma_start(sorted_edges[s].rearrange("(l w) o -> l (w o)", l=LANES), sentinel).then_inc(prefilled, 16)
            sp.dma_start(xs[:, 0:NB - 1, :], x[0:(NB - 1) * P, :].rearrange("(b p) f -> p b f", p=P)).then_inc(inputs_in, 16)
            sp.dma_start(xs[0:NLAST, NB - 1, :], x[(NB - 1) * P:N, :]).then_inc(inputs_in, 16)
            for a, d in ((w_s, w), (qw_s, q_w), (kw_s, k_w), (emb_s, emb)):
                sp.dma_start(a[:], d).then_inc(inputs_in, 16)
            for a, d in ((al_s, attn_l.rearrange("a b -> (a b)")), (ar_s, attn_r.rearrange("a b -> (a b)")), (bias_s, bias), (gamma_s, gamma), (beta_s, beta)):
                sp.dma_start(a[:], d.partition_broadcast(P)).then_inc(inputs_in, 16)

            for s in range(2):
                sp.wait_ge(meta_ready, s + 1)
                sp.dma_start(meta_d[s].rearrange("p g c -> p (g c)"), (wide[:, 0:NG * MW], tmp_meta)[s]).then_inc(meta_stored, 16)
                sp.wait_ge(positions_ready, s + 1)

                def stage_chunk(i, h, first):
                    if not first:
                        sp.wait_ge(scattered[h], sp.snap(i * (16 * CH) + (s * CHUNKS) * 16 * CH))
                        apart(sp)
                    at = i * (2 * CH) + h * CH
                    sp.dma_start(stage[:, h, 0, :], pos_i[s][:, bass.ds(at, CH)]).then_inc(staged[h], 16)
                    sp.dma_start(stage[:, h, 1, :], packed[:, bass.ds(at, CH)]).then_inc(staged[h], 16)

                for h in range(2):
                    stage_chunk(0, h, s == 0)
                with sp.Fori(1, CHUNKS) as i:
                    for h in range(2):
                        stage_chunk(i, h, False)
            for s in range(2):
                if s == 0:
                    for h in range(2):
                        sp.wait_ge(scattered[h], 2 * CHUNKS * 16 * CH)
                else:
                    sp.wait_ge(decoded, 1)
                sp.dma_start(s_packed, sorted_edges[s].rearrange("(l w) o -> l (w o)", l=LANES)).then_inc(resorted_in, 16)
                sp.wait_ge(decoded, s + 1)
                sp.dma_start(key_d[s].rearrange("(l w) -> l w", l=LANES), s_key).then_inc(sorted_stored, 16)
                if s == 1:
                    sp.dma_start(type_d.rearrange("(l w) -> l w", l=LANES), s_type16).then_inc(sorted_stored, 16)
            sp.wait_ge(feat_whole, 1)
            sp.dma_start(feat_d.rearrange("(b p) c -> p b c", p=P), feat).then_inc(feat_stored, 16)
            sp.dma_start(er_d.rearrange("b p h -> p b h"), er[:]).then_inc(feat_stored, 16)
            sp.wait_ge(meta_stored, 32)
            sp.wait_ge(sorted_stored, 3 * 16)
            sp.wait_ge(feat_stored, 32)
            sp.wait_ge(pipes_free, 1)

            def load_store(layer):
                q = pipes[layer]

                def step(b, k):
                    j = k
                    if not b.last and k % R == 0:
                        if not b.first:
                            sp.wait_ge(q["off_done"], b.count(j - R - 1))
                            apart(sp)
                            sp.wait_ge(q["gathered"][(j - R - 1) % R], b.landed("gathered", j - R - 1))
                            apart(sp)
                        g = b.at + k
                        d = q["unit"][j // R]
                        at = (lambda a, n: a[:, g * n:(g + R) * n] if b.first else a[:, bass.ds(g * n, R * n)])
                        row = (lambda a: a[g * G:(g + R) * G] if b.first else a[bass.ds(g * G, R * G)])
                        flat = (lambda a: a[:, k:k + R, :].rearrange("p a b -> p (a b)"))
                        sp.dma_start(flat(peer_r), at(peers[layer], 2)).then_inc(d, 16)
                        sp.dma_start(flat(key_r), row(key_d[layer]).partition_broadcast(P)).then_inc(d, 16)
                        sp.dma_start(flat(unit_meta), at(meta_d[layer].rearrange("p g c -> p (g c)"), MW)).then_inc(d, 16)
                        if layer == 1:
                            sp.dma_start(flat(type_r)[0:RELS], row(type_d).partition_broadcast(RELS)).then_inc(d, 16)
                    if not b.last:
                        if not b.first:
                            sp.wait_ge(q["relu_done" if layer == 0 else "scores_ready"], b.count(j - U))
                            apart(sp)
                        g = b.at + k
                        blk = sp.value_load(plan[layer][0:1, g:g + 1] if b.first else plan[layer][0:1, bass.ds(g, 1)],
                                            min_val=0, max_val=NB - 1)
                        if layer == 0:
                            sp.dma_start(er_r[:, j % U, :], er_d[bass.ds(blk, 1)].rearrange("o p c -> p (o c)")).then_inc(q["block"][j % U], 16)
                        else:
                            sp.dma_start(left_r[:, j % U, :], left_d[bass.ds(blk, 1)].rearrange("o f n -> f (o n)")).then_inc(q["block"][j % U], 16)
                    j = k - STORE[layer]
                    if b.has(j) and j % R == R - 1:
                        sp.wait_ge(q["acc_done"], b.count(j))
                        apart(sp)
                        g = b.at + (j - R + 1)
                        to = state_d[:, g * SW:(g + R) * SW] if isinstance(g, int) else state_d[:, bass.ds(g * SW, R * SW)]
                        sp.dma_start(to, acc_r[:, (j - R + 1) % U:j % U + 1, :].rearrange("p a b -> p (a b)")).then_inc(q["stored"][(j // R) % 2], 16)
                return step

            def load_states(layer):
                apart(sp)
                with sp.Fori(0, NB) as b:
                    g = sp.value_load(lastg[layer][0:1, bass.ds(b, 1)], min_val=0, max_val=NG - 1)
                    sp.dma_start(wide[:, bass.ds(b * SW, SW)], state_d[:, bass.ds(g * SW, SW)]).then_inc(state_in, 16)

            pipeline(sp, None, load_store(0), uses[0])
            for i in range(2):
                sp.wait_ge(pipes[0]["stored"][i], 16 * BODIES)
            load_states(0)

            with sp.Fori(0, HOPS) as hop:
                sp.wait_ge(agg_ready, hop + 1)
                sp.dma_start(agg_d.rearrange("(b p) f -> p b f", p=P), agg[:]).then_inc(hop_stored, 16)
                sp.wait_ge(left_copied, sp.snap(hop * LB + LB))
                sp.dma_start(left_d.rearrange("b f n -> f b n"), left).then_inc(hop_stored, 16)
                sp.wait_ge(hop_stored, sp.snap(hop * 32 + 32))
                pipeline(sp, hop, load_store(1), uses[1])
                for i in range(2):
                    sp.wait_ge(pipes[1]["stored"][i], sp.snap(hop * (16 * BODIES) + 16 * BODIES))
                load_states(1)
                sp.wait_ge(hop_done, hop + 1)
                apart(sp)
            sp.wait_ge(out_ready, 1)
            sp.dma_start(out[0:(NB - 1) * P, :].rearrange("(b p) f -> p b f", p=P), xs[:, 0:NB - 1, :]).then_inc(out_stored, 16)
            sp.dma_start(out[(NB - 1) * P:N, :], xs[0:NLAST, NB - 1, :]).then_inc(out_stored, 16)
            sp.wait_ge(out_stored, 32)

        @block.gpsimd
        def _(pool):
            nc.gpsimd.iota(giota[:], [[1, NG]], base=0, channel_multiplier=0, allow_small_or_imprecise_dtypes=True)
            nc.gpsimd.iota(biota[:], [[1, 64]], base=0, channel_multiplier=0, allow_small_or_imprecise_dtypes=True)
            nc.gpsimd.iota(rowid[:], [[0, P]], base=0, channel_multiplier=1, allow_small_or_imprecise_dtypes=True)
            nc.gpsimd.iota(colid[:], [[1, P]], base=0, channel_multiplier=0, allow_small_or_imprecise_dtypes=True).then_inc(rowid_made, 1)

            pool.wait_ge(prefilled, 32)
            for s in range(2):
                with pool.Fori(0, CHUNKS) as i:
                    for h in range(2):
                        pool.wait_ge(staged[h], pool.snap(i * 32 + (s * CHUNKS + 1) * 32))
                        apart(pool)
                        for c in range(CH):
                            nc.gpsimd.indirect_dma_start(
                                out=sorted_edges[s], out_offset=bass.IndirectOffsetOnAxis(ap=stage[:, h, 0, c:c + 1], axis=0),
                                in_=stage[:, h, 1, c:c + 1], in_offset=None, bounds_check=NG * G - 1, oob_is_err=False,
                            ).then_inc(scattered[h], 16)

            def gather(layer):
                q = pipes[layer]
                table = (feat_d, agg_d)[layer]
                width = (TW, F)[layer]

                def step(b, k):
                    if b.last:
                        return
                    pool.wait_ge(q["unit"][k // R], b.landed("unit", k))
                    if not (b.first and k < R):
                        pool.wait_ge(q["sum_ready" if layer == 0 else "val_done"], b.count(k - R))
                    apart(pool)
                    for c in range(2):
                        nc.gpsimd.indirect_dma_start(
                            out=rows_r[:, k % R, c, 0:width], out_offset=None, in_=table,
                            in_offset=bass.IndirectOffsetOnAxis(ap=peer_r[:, k, c:c + 1], axis=0),
                        ).then_inc(q["gathered"][k % R], 16)
                return step

            pool.wait_ge(feat_stored, 32)
            pipeline(pool, None, gather(0), uses[0])
            with pool.Fori(0, HOPS) as hop:
                pool.wait_ge(hop_stored, pool.snap(hop * 32 + 32))
                apart(pool)
                pipeline(pool, hop, gather(1), uses[1])

        @block.tensor
        def _(pe):
            def mm(out, lhsT, rhs, start=True, stop=True):
                return nc.tensor.matmul(out, lhsT, rhs, start=start, stop=stop)

            pe.wait_ge(consts_made, 1)
            for s in range(2):
                pe.wait_ge(counts_ready, s + 1)
                mm(bank[0][:, 0:NB], before[:], counts[:])
                mm(bank[1][:, 0:NB], ones[:], counts[:])
                mm(bank[2][0:NB, 0:1], counts[:], ones[:, 0:1]).then_inc(totals_ready, 1)
                pe.wait_ge(groups_ready, s + 1)
                mm(bank[4][0:NB, 0:1], upto[0:NB, 0:NB], few[0:NB, 1:2]).then_inc(ends_ready, 1)
                pe.wait_ge(member_ready, s + 1)
                for h in range(2):
                    last = mm(bank[5 + h][:, 0:NG // 2], rowid[0:NB, :], member[0:NB, h * (NG // 2):(h + 1) * (NG // 2)])
                last.then_inc(blocks_ready, 1)

            pe.wait_ge(hidden_ready, 1)
            pe.wait_ge(weights_ready, 1)
            for t in range(FB + 1):
                if t < FB:
                    if t >= 2:
                        pe.wait_ge(hiddenT_copied, t - 1)
                    for i in range(min(3, NB - 3 * t)):
                        last = nc.tensor.transpose(bank[t % 2][:, i * P:(i + 1) * P], agg[:, 3 * t + i, :], ident[:])
                    last.then_inc(hiddenT_ready, 1)
                if t >= 1:
                    pe.wait_ge(hiddenT_copied, t)
                    if t >= 3:
                        pe.wait_ge(feat_copied, t - 2)
                    for i in range(min(3, NB - 3 * (t - 1))):
                        last = mm(bank[2 + (t - 1) % 2][:, i * (TW + HEADS):(i + 1) * (TW + HEADS)],
                                  batchT[:, (t - 1) % 2, i * P:(i + 1) * P], wx[:])
                    last.then_inc(feat_ready, 1)

            for s in range(2):
                for t in range(U):
                    if t == 0:
                        pe.wait_ge(decoded, s + 1)
                    if s * U + t >= 4:
                        pe.wait_ge(peerT_copied, s * U + t - 3)
                    nc.tensor.transpose(bank[4 + t % 4 if s == 0 else 4 + (t + U) % 4][:, 0:LANES], s_peer[:, t * P:(t + 1) * P],
                                        ident[0:LANES, 0:LANES]).then_inc(peerT_ready, 1)
            q = pipes[0]

            def attn_step(b, k):
                j = k - 5
                if b.has(j):
                    pe.wait_ge(q["gathered"][j % R], b.landed("gathered", j))
                    if not (b.first and j < 2):
                        pe.wait_ge(q["neg_done"], b.count(j - 2))
                    elif b.first and j == 0:
                        pe.wait_ge(feat_whole, 1)
                    for h in range(HEADS):
                        for c in range(2):
                            last = nc.tensor.transpose(
                                bank[j % 2][:, h * G + c * P:h * G + (c + 1) * P],
                                rows_r[:, j % R, c, h * (FH + 2) + FH + 1:h * (FH + 2) + FH + 2].to_broadcast([P, P]), ident[:])
                    last.then_inc(q["scores_ready"], 1)
                j = k - 7
                if b.has(j):
                    pe.wait_ge(q["exp_done"], b.count(j))
                    for i in range(2 * HEADS):
                        last = nc.tensor.transpose(bank[2 + j % 2][:, i * P:(i + 1) * P], prob_r[:, j % 2, i * P:(i + 1) * P], ident[:])
                    last.then_inc(q["probT_ready"], 1)
                j = k - 8
                if b.has(j):
                    if not (b.first and j < 2):
                        pe.wait_ge(q["acc_done"], b.count(j - 2))
                    pe.wait_ge(q["probT_copied"], b.count(j))
                    for h in range(HEADS):
                        for c in range(2):
                            last = mm(bank[4 + j % 2][:, h * (FH + 1):(h + 1) * (FH + 1)], probT_r[:, j % R, 2 * h + c, :],
                                      rows_r[:, j % R, c, h * (FH + 2):h * (FH + 2) + FH + 1], c == 0, c == 1)
                    last.then_inc(q["sum_ready"], 1)

            pipeline(pe, None, attn_step, uses[0])

            h_ = pipes[1]

            def hop_pe_step(b, k):
                q = h_
                j = k - 11
                if b.has(j):
                    if not (b.first and j < 2):
                        pe.wait_ge(q["acc_done"], b.count(j - 2))
                    pe.wait_ge(q["probT_copied"], b.count(j))
                    for c in range(2):
                        last = mm(bank[5 + j % 2][:, 0:F + 1], probT_r[:, j % R, c, :], val_r[:, j % R, c, :], c == 0, c == 1)
                    last.then_inc(q["sum_ready"], 1)
                j = k - 10
                if b.has(j):
                    pe.wait_ge(q["exp_done"], b.count(j))
                    for c in range(2):
                        last = nc.tensor.transpose(bank[4][:, c * P:(c + 1) * P], prob_r[:, j % 2, c * P:(c + 1) * P], ident[:])
                    last.then_inc(q["probT_ready"], 1)
                j = k - 8
                if b.has(j):
                    pe.wait_ge(q["block"][j % U], b.landed("block", j))
                    pe.wait_ge(q["right_done"], b.count(j))
                    mm(bank[(3, 7)[j % 2]][:, 0:G], left_r[:, j % U, :], right_r[:, j % R, :]).then_inc(q["scores_ready"], 1)
                j = k - 7
                if b.has(j):
                    pe.wait_ge(q["valT_copied"], b.count(j))
                    mm(bank[2][:, 0:G], kw_s[:], valT_r[:, j % R, :]).then_inc(q["right_ready"], 1)
                j = k - 6
                if b.has(j):
                    pe.wait_ge(q["val_done"], b.count(j))
                    for c in range(2):
                        last = nc.tensor.transpose(bank[1][:, c * P:(c + 1) * P], val_r[:, j % R, c, 0:F], ident[:])
                    last.then_inc(q["valT_ready"], 1)
                j = k - 5
                if b.has(j):
                    pe.wait_ge(q["off_done"], b.count(j))
                    for c in range(2):
                        for i in range(3):
                            last = mm(bank[0][:, c * P:(c + 1) * P], hot_r[0:RELS, j % R, c * P:(c + 1) * P], emb3[:, i, :], i == 0, i == 2)
                    last.then_inc(q["rel_ready"], 1)

            with pe.Fori(0, HOPS) as hop:
                pe.wait_ge(agg_ready, hop + 1)
                tiles = pe.snap(hop * LB)
                for t in range(LB + 1):
                    if t < LB:
                        if t >= 2:
                            pe.wait_ge(aggT_copied, tiles + (t - 1))
                        for i in range(min(4, NB - 4 * t)):
                            last = nc.tensor.transpose(bank[t % 2][:, i * P:(i + 1) * P], agg[:, 4 * t + i, :], ident[:])
                        last.then_inc(aggT_ready, 1)
                    if t >= 1:
                        pe.wait_ge(aggT_copied, tiles + t)
                        if t >= 3:
                            pe.wait_ge(left_copied, tiles + (t - 2))
                        n = min(4, NB - 4 * (t - 1)) * P
                        mm(bank[2 + (t - 1) % 2][:, 0:n], qw_s[:], batchT[:, (t - 1) % 2, 0:n]).then_inc(left_ready, 1)
                pe.wait_ge(left_copied, tiles + LB)
                pipeline(pe, hop, hop_pe_step, uses[1])

        @block.scalar
        def _(act):
            def root(n):
                act.wait_ge(var_ready, n)
                nc.scalar.activation(stat[2][:, :, 0:1], stat[1][:, :, 0:1], ACT.Sqrt).then_inc(std_ready, 1)

            root(1)
            for t in range(FB):
                act.wait_ge(hiddenT_ready, t + 1)
                if t >= 2:
                    act.wait_ge(feat_ready, t - 1)
                n = min(3, NB - 3 * t) * P
                nc.scalar.copy(batchT[:, t % 2, 0:n], bank[t % 2][:, 0:n]).then_inc(hiddenT_copied, 1)
            q = pipes[0]

            def attn_step(b, k):
                j = k - 7
                if b.has(j):
                    act.wait_ge(q["min_done"], b.count(j))
                    for h in range(HEADS):
                        nc.scalar.activation(alpha_r[:, j % R, h:h + 1], min_r[:, j % R, h:h + 1], ACT.Exp, bias=fade_r[:, j % R, h:h + 1])
                    for h in range(HEADS):
                        last = nc.scalar.activation(prob_r[:, j % 2, h * G:(h + 1) * G], score_r[:, j % R, h * G:(h + 1) * G],
                                                    ACT.Exp, scale=-1.0, bias=min_r[:, j % R, h:h + 1])
                    last.then_inc(q["exp_done"], 1)
                j = k - 5
                if b.has(j):
                    act.wait_ge(q["block"][j % U], b.landed("block", j))
                    act.wait_ge(q["scores_ready"], b.count(j))
                    for h in range(HEADS):
                        last = nc.scalar.activation(relu_r[:, j % 2, h * G:(h + 1) * G], bank[j % 2][:, h * G:(h + 1) * G],
                                                    ACT.Relu, scale=1.0 - SLOPE, bias=er_r[:, j % U, h:h + 1])
                    last.then_inc(q["relu_done"], 1)
                j = k - 7
                if b.has(j):
                    act.wait_ge(q["probT_ready"], b.count(j))
                    nc.scalar.copy(probT_r[:, j % R, :, :], bank[2 + j % 2][:].rearrange("p (a b) -> p a b", b=P)).then_inc(q["probT_copied"], 1)

            pipeline(act, None, attn_step, uses[0])
            root(2)
            root(3)
            h_ = pipes[1]

            def hop_act_step(b, k):
                q = h_
                j = k - 9
                if b.has(j):
                    act.wait_ge(q["min_done"], b.count(j))
                    nc.scalar.activation(prob_r[:, j % 2, 0:G], score_r[:, j % R, 0:G], ACT.Exp, scale=-1.0,
                                         bias=min_r[:, j % R, 0:1]).then_inc(q["exp_done"], 1)
                    nc.scalar.activation(alpha_r[:, j % R, 0:1], min_r[:, j % R, 0:1], ACT.Exp, bias=fade_r[:, j % R, 0:1])
                    nc.scalar.activation(nohit_r[:, j % R, :], off_r[:, j % R, :], ACT.Exp, scale=-1.0, accum_out=cnt_r[:, j % R, 0:1])
                j = k - 10
                if b.has(j):
                    act.wait_ge(q["probT_ready"], b.count(j))
                    nc.scalar.copy(probT_r[:, j % R, 0:2, :], bank[4][:, 0:G].rearrange("p (a b) -> p a b", b=P)).then_inc(q["probT_copied"], 1)
                j = k - 7
                if b.has(j):
                    act.wait_ge(q["right_ready"], b.count(j))
                    nc.scalar.activation(right_r[:, j % R, :], bank[2][:, 0:G], ACT.Tanh).then_inc(q["right_done"], 1)
                j = k - 6
                if b.has(j):
                    act.wait_ge(q["valT_ready"], b.count(j))
                    nc.scalar.copy(valT_r[:, j % R, :], bank[1][:, 0:G]).then_inc(q["valT_copied"], 1)

            with act.Fori(0, HOPS) as hop:
                tiles = act.snap(hop * LB)
                for t in range(LB):
                    act.wait_ge(aggT_ready, tiles + (t + 1))
                    if t >= 2:
                        act.wait_ge(left_ready, tiles + (t - 1))
                    n = min(4, NB - 4 * t) * P
                    nc.scalar.copy(batchT[:, t % 2, 0:n], bank[t % 2][:, 0:n]).then_inc(aggT_copied, 1)
                pipeline(act, hop, hop_act_step, uses[1])
                act.wait_ge(var_ready, hop + 4)
                nc.scalar.activation(stat[2][:, :, 0:1], stat[1][:, :, 0:1], ACT.Sqrt).then_inc(std_ready, 1)

        @block.vector
        def _(dve):
            V = nc.vector
            steps = [0]

            def do(ins):
                ins.then_inc(dve_step, 1)
                steps[0] += 1
                dve.wait_ge(dve_step, steps[0])

            def signal(s):
                dve.sem_inc(s, 1)

            for a in (src_i, dst_i, type_i):
                V.memset(a, PADKEY)
            V.memset(sentinel, PADKEY << SHIFT | PADKEY)
            V.memset(xs[:], 0.0)
            V.memset(wx[:], 0.0).then_inc(pads_set, 1)
            do(V.memset(ones[:], 1.0))
            dve.wait_ge(rowid_made, 1)
            V.tensor_tensor(ident[:], rowid[:], colid[:], ALU.is_equal)
            V.tensor_tensor(before[:], rowid[:], colid[:], ALU.is_lt)
            V.tensor_tensor(upto[:], rowid[:], colid[:], ALU.is_le).then_inc(consts_made, 1)
            dve.wait_ge(edges_in, 6 * 16)

            def find_positions(s):
                key = (dst_i, src_i)[s]
                if s == 1:
                    for h in range(2):
                        dve.wait_ge(scattered[h], CHUNKS * 16 * CH)
                do(V.tensor_scalar(spare_i, key, 7, None, ALU.logical_shift_right))
                do(V.tensor_copy(high, spare_i))
                with dve.Fori(0, NB) as b:
                    n = dve.snap(b + s * NB)
                    dve.wait_ge(count_step, n)
                    V.tensor_scalar(mask.bitcast(BF16), high, biota[:, bass.ds(b, 1)], None, ALU.is_equal, ALU.add,
                                    accum_out=counts[:, bass.ds(b, 1)]).then_inc(count_step, 1)
                dve.wait_ge(count_step, (s + 1) * NB)
                signal(counts_ready)
                dve.wait_ge(totals_ready, s + 1)
                do(V.tensor_copy(few[0:NB, 0:1], bank[2][0:NB, 0:1]))
                do(V.tensor_scalar(few[0:NB, 2:3], few[0:NB, 0:1], float(G - 1), None, ALU.add))
                do(V.tensor_copy(fewi[0:NB, 0:1], few[0:NB, 2:3]))
                do(V.tensor_scalar(fewi[0:NB, 1:2], fewi[0:NB, 0:1], G.bit_length() - 1, None, ALU.logical_shift_right))
                do(V.tensor_copy(few[0:NB, 3:4], fewi[0:NB, 1:2]))
                do(V.tensor_scalar(few[0:NB, 1:2], few[0:NB, 3:4], 1.0, None, ALU.max))
                signal(groups_ready)
                do(V.tensor_scalar(rows[0][:], bank[1][:, 0:NB], float(G - 1), None, ALU.add))
                do(V.tensor_copy(rowsi[:], rows[0][:]))
                do(V.tensor_scalar(rowsi2[:], rowsi[:], G.bit_length() - 1, None, ALU.logical_shift_right))
                do(V.tensor_copy(rows[0][:], rowsi2[:]))
                do(V.tensor_scalar(rows[1][:], rows[0][:], 1.0, None, ALU.max))
                do(V.tensor_tensor_scan(rows[2][:], ones[:, 0:NB], rows[1][:], 0.0, ALU.mult, ALU.add))
                do(V.tensor_scalar(lastg[s][:], rows[2][:], -1.0, None, ALU.add))
                do(V.tensor_tensor(rows[0][:], rows[2][:], rows[1][:], ALU.subtract))
                do(V.scalar_tensor_tensor(rows[3][:], rows[0][:], float(G), bank[0][:, 0:NB], ALU.mult, ALU.add))
                dve.wait_ge(ends_ready, s + 1)
                do(V.tensor_copy(few[0:NB, 4:5], bank[4][0:NB, 0:1]))
                do(V.tensor_tensor(few[0:NB, 5:6], few[0:NB, 4:5], few[0:NB, 1:2], ALU.subtract))
                do(V.tensor_scalar(few[0:NB, 7:8], rowid[0:NB, 0:1], float(NB - 1), 1e6, ALU.is_equal, ALU.mult))
                do(V.tensor_tensor(few[0:NB, 8:9], few[0:NB, 7:8], few[0:NB, 4:5], ALU.add))
                do(V.tensor_scalar(scratch[0][0:NB, :], giota[0:NB, :], few[0:NB, 5:6], None, ALU.is_ge))
                do(V.scalar_tensor_tensor(member[0:NB, :], giota[0:NB, :], few[0:NB, 8:9], scratch[0][0:NB, :], ALU.is_lt, ALU.mult))
                signal(member_ready)
                dve.wait_ge(blocks_ready, s + 1)
                half_g = NG // 2
                for h in range(2):
                    do(V.tensor_copy(scratch[1][:, h * half_g:(h + 1) * half_g], bank[5 + h][:, 0:half_g]))
                do(V.tensor_copy(plan[s][:], scratch[1]))
                meta = (wide[:, 0:NG * MW], tmp_meta)[s].rearrange("p (g c) -> p g c", c=MW)
                m = [meta[:, :, i] for i in range(MW)]
                if s == 0:
                    dve.wait_ge(prefilled, 32)
                do(V.memset(meta, 0.0))
                do(V.tensor_tensor(m[KEEP][:, 1:NG], scratch[1][:, 1:NG], scratch[1][:, 0:NG - 1], ALU.is_equal))
                do(V.tensor_scalar(m[RESET], m[KEEP], -0.5 * BIG, 0.5 * BIG, ALU.mult, ALU.add))
                do(V.tensor_scalar(m[NKEEP], m[KEEP], -1.0, None, ALU.mult))
                do(V.tensor_scalar(m[FORGET], m[KEEP], 0.75 * BIG, -0.75 * BIG, ALU.mult, ALU.add))
                do(V.tensor_scalar(m[TARGET], scratch[1], float(P), rowid[:, 0:1], ALU.mult, ALU.add))
                signal(meta_ready)
                do(V.memset(pos_f, NOWHERE))
                with dve.Fori(0, NB) as b:
                    n = dve.snap(b * 3 + s * 3 * NB)
                    dve.wait_ge(bucket_step, n)
                    V.tensor_scalar(mask, high, biota[:, bass.ds(b, 1)], None, ALU.is_equal).then_inc(bucket_step, 1)
                    dve.wait_ge(bucket_step, n + 1)
                    V.tensor_tensor_scan(run_f, ones[:, 0:1].to_broadcast([P, COLS]), mask, rows[3][:, bass.ds(b, 1)], ALU.mult, ALU.add).then_inc(bucket_step, 1)
                    dve.wait_ge(bucket_step, n + 2)
                    apart(dve)
                    V.copy_predicated(pos_f, mask, run_f).then_inc(bucket_step, 1)
                dve.wait_ge(bucket_step, (s + 1) * 3 * NB)
                do(V.tensor_scalar(pos_i[s], pos_f, -1.0, None, ALU.add))
                if s == 0:
                    do(V.tensor_scalar(spare_i, type_i, 2 * SHIFT, None, ALU.logical_shift_left))
                    do(V.tensor_scalar(packed, dst_i, SHIFT, None, ALU.logical_shift_left))
                    do(V.tensor_tensor(spare_i, spare_i, packed, ALU.bitwise_or))
                    do(V.tensor_tensor(packed, spare_i, src_i, ALU.bitwise_or))
                signal(positions_ready)

            find_positions(0)
            find_positions(1)

            def norm(src_t, dst_t, n):
                do(V.reduce_sum(stat[0][:, :, 0], src_t, axis=AX))
                do(V.tensor_scalar(stat[0][:, :, 1], stat[0][:, :, 0], 1.0 / F, None, ALU.mult))
                do(V.tensor_tensor(tmp[:], src_t, stat[0][:, :, 1:2].to_broadcast([P, NB, F]), ALU.subtract))
                do(V.tensor_tensor(dst_t, tmp[:], tmp[:], ALU.mult))
                do(V.reduce_sum(stat[1][:, :, 1], dst_t, axis=AX))
                do(V.tensor_scalar(stat[1][:, :, 0], stat[1][:, :, 1], 1.0 / F, EPS, ALU.mult, ALU.add))
                signal(var_ready)
                dve.wait_ge(std_ready, n)
                do(V.reciprocal(stat[2][:, :, 1], stat[2][:, :, 0]))
                do(V.tensor_tensor(dst_t, tmp[:], stat[2][:, :, 1:2].to_broadcast([P, NB, F]), ALU.mult))

            dve.wait_ge(inputs_in, 11 * 16)
            for h in range(HEADS):
                c0 = h * (FH + 2)
                do(V.tensor_copy(wx[:, c0:c0 + FH], w_s[:, h * FH:(h + 1) * FH]))
                do(V.tensor_tensor(junk[:], w_s[:, h * FH:(h + 1) * FH], al_s[:, h * FH:(h + 1) * FH], ALU.mult))
                do(V.reduce_sum(wx[:, c0 + FH + 1:c0 + FH + 2], junk[:], axis=AX))
                do(V.tensor_tensor(junk[:], w_s[:, h * FH:(h + 1) * FH], ar_s[:, h * FH:(h + 1) * FH], ALU.mult))
                do(V.reduce_sum(wx[:, TW + h:TW + h + 1], junk[:], axis=AX))
            do(V.tensor_copy(emb3[:, 0, :], emb_s[:]))
            do(V.tensor_tensor(emb_rest[:], emb_s[:], emb3[:, 0, :], ALU.subtract))
            do(V.tensor_copy(emb3[:, 1, :], emb_rest[:]))
            do(V.tensor_tensor(emb_s[:], emb_rest[:], emb3[:, 1, :], ALU.subtract))
            do(V.tensor_copy(emb3[:, 2, :], emb_s[:]))
            signal(weights_ready)

            dve.wait_ge(meta_stored, 32)
            norm(xs[:], agg[:], 1)
            do(V.tensor_scalar(agg[:], agg[:], 0.0, None, ALU.max))
            signal(hidden_ready)
            for t in range(FB):
                dve.wait_ge(feat_ready, t + 1)
                k = min(3, NB - 3 * t)
                s_ = bank[2 + t % 2][:, 0:k * (TW + HEADS)].rearrange("p (b c) -> p b c", b=k)
                V.tensor_copy(feat[:, 3 * t:3 * t + k, :], s_[:, :, 0:TW])
                V.tensor_scalar(er[:, 3 * t:3 * t + k, :], s_[:, :, TW:TW + HEADS], 1.0 - SLOPE, None, ALU.mult).then_inc(feat_copied, 1)
            dve.wait_ge(feat_copied, FB)
            for h in range(HEADS):
                do(V.memset(feat[:, :, h * (FH + 2) + FH:h * (FH + 2) + FH + 1], 1.0))
            signal(feat_whole)

            for s in range(2):
                dve.wait_ge(resorted_in, (s + 1) * 16)
                if s == 1:
                    dve.wait_ge(sorted_stored, 16)
                do(V.tensor_scalar(s_src, s_packed, MASK, None, ALU.bitwise_and))
                do(V.tensor_scalar(s_part, s_packed, SHIFT, None, ALU.logical_shift_right))
                do(V.tensor_scalar(s_dst, s_part, MASK, None, ALU.bitwise_and))
                do(V.tensor_scalar(s_type, s_packed, 2 * SHIFT, None, ALU.logical_shift_right))
                do(V.tensor_copy(s_key, (s_dst, s_src)[s]))
                do(V.tensor_copy(s_type16, s_type))
                do(V.tensor_scalar(s_peer, (s_src, s_dst)[s], float(N - 1), None, ALU.min))
                signal(decoded)
                by_lane = peers[s][:].rearrange("p (l t) -> p l t", t=U)
                for t in range(U):
                    dve.wait_ge(peerT_ready, s * U + t + 1)
                    V.tensor_copy(by_lane[:, :, t], bank[4 + (s * U + t) % 4][:, 0:LANES]).then_inc(peerT_copied, 1)
                dve.wait_ge(peerT_copied, (s + 1) * U)
            dve.wait_ge(sorted_stored, 3 * 16)
            do(V.memset(acc_r, 0.0))
            do(V.memset(min_r, 0.0))
            signal(pipes_free)
            dve.wait_ge(feat_stored, 32)

            q0 = pipes[0]

            def masks(q, b, j, layer):
                dve.wait_ge(q["unit"][(j // R) % 2], b.landed("unit", j))
                V.tensor_copy(meta_r[:, j % U, :], unit_meta[:, j % U, :])
                if layer == 1:
                    V.tensor_scalar(hot_r[0:RELS, j % R, :], type_r[0:RELS, j % U, :], rowid[0:RELS, 0:1], None, ALU.is_equal)
                V.tensor_scalar(off_r[:, j % R, :], key_r[:, j % U, :], unit_meta[:, j % U, TARGET:TARGET + 1], BIG,
                                ALU.not_equal, ALU.mult).then_inc(q["off_done"], 1)

            def start_min(q, b, j, n):
                m = meta_r[:, j % U, :]
                dve.wait_ge(q["off_done"], b.count(j))
                if not (b.first and j == 0):
                    dve.wait_ge(q["min_done"], b.count(j - 1))
                V.tensor_scalar(min_in_r[:, j % R, 0:n], min_r[:, (j - 1) % R, 0:n], m[:, KEEP:KEEP + 1], m[:, RESET:RESET + 1], ALU.mult, ALU.add)
                V.tensor_scalar(fade_r[:, j % R, 0:n], min_r[:, (j - 1) % R, 0:n], m[:, NKEEP:NKEEP + 1], m[:, FORGET:FORGET + 1],
                                ALU.mult, ALU.add).then_inc(q["min_in_done"], 1)

            def accumulate(q, b, j):
                dve.wait_ge(q["sum_ready"], b.count(j))
                if not (b.first and j == 0):
                    dve.wait_ge(q["acc_done"], b.count(j - 1))
                if j % R == 0 and not (b.first and j < U):
                    dve.wait_ge(q["stored"][(j // R) % 2], b.landed("stored", j - U))

            def attn_step(b, k):
                q = q0
                j = k - 9
                if b.has(j):
                    accumulate(q, b, j)
                    for h in range(HEADS):
                        c = slice(h * (FH + 1), (h + 1) * (FH + 1))
                        last = V.scalar_tensor_tensor(acc_r[:, j % U, c], acc_r[:, (j - 1) % U, c], alpha_r[:, j % R, h:h + 1],
                                                      bank[4 + j % 2][:, c], ALU.mult, ALU.add)
                    last.then_inc(q["acc_done"], 1)
                j = k - 6
                if b.has(j):
                    start_min(q, b, j, HEADS)
                    dve.wait_ge(q["relu_done"], b.count(j))
                    V.scalar_tensor_tensor(score_r[:, j % R, :], bank[j % 2][:], -SLOPE, relu_r[:, j % 2, :], ALU.mult, ALU.subtract).then_inc(q["neg_done"], 1)
                j = k - 4
                if b.has(j):
                    masks(q, b, j, 0)
                j = k - 6
                if b.has(j):
                    dve.wait_ge(q["min_in_done"], b.count(j))
                    dve.wait_ge(q["neg_done"], b.count(j))
                    apart(dve)
                    for h in range(HEADS):
                        last = V.tensor_tensor_reduce(out=score_r[:, j % R, h * G:(h + 1) * G], in0=score_r[:, j % R, h * G:(h + 1) * G],
                                                      in1=off_r[:, j % R, :], scale=1.0, scalar=min_in_r[:, j % R, h:h + 1],
                                                      op0=ALU.add, op1=ALU.min, accum_out=min_r[:, j % R, h:h + 1])
                    last.then_inc(q["min_done"], 1)

            pipeline(dve, None, attn_step, uses[0])

            dve.wait_ge(state_in, NB * 16)
            st = state.rearrange("p b (h c) -> p b h c", h=HEADS)
            do(V.tensor_scalar(stat[0][:], st[:, :, :, FH], 1e-30, None, ALU.max))
            do(V.reciprocal(stat[1][:], stat[0][:]))
            for h in range(HEADS):
                do(V.tensor_tensor(agg[:, :, h * FH:(h + 1) * FH], st[:, :, h, 0:FH], stat[1][:, :, h:h + 1].to_broadcast([P, NB, FH]), ALU.mult))
            every = lambda a: a[:].rearrange("p (o f) -> p o f", o=1).to_broadcast([P, NB, F])
            do(V.tensor_tensor(agg[:], agg[:], every(bias_s), ALU.add))
            norm(agg[:], agg[:], 2)
            do(V.tensor_tensor(agg[:], agg[:], every(gamma_s), ALU.mult))
            do(V.tensor_tensor(agg[:], agg[:], every(beta_s), ALU.add))
            do(V.tensor_tensor(xs[:], xs[:], agg[:], ALU.add))
            norm(xs[:], agg[:], 3)
            do(V.tensor_scalar(agg[:], agg[:], 0.0, None, ALU.max))
            do(V.scalar_tensor_tensor(xs[:], agg[:], float(HOPS), xs[:], ALU.mult, ALU.add))
            do(V.memset(val_r, 1.0))
            do(V.memset(acc_r, 0.0))
            signal(agg_ready)
            q1 = pipes[1]

            def hop_dve_step(b, k):
                q = q1
                j = k - 12
                if b.has(j):
                    accumulate(q, b, j)
                    V.tensor_scalar(acc_r[:, j % U, F + 1:F + 2], acc_r[:, (j - 1) % U, F + 1:F + 2], meta_r[:, j % U, KEEP:KEEP + 1],
                                    cnt_r[:, j % R, 0:1], ALU.mult, ALU.add)
                    V.scalar_tensor_tensor(acc_r[:, j % U, 0:F + 1], acc_r[:, (j - 1) % U, 0:F + 1], alpha_r[:, j % R, 0:1],
                                           bank[5 + j % 2][:, 0:F + 1], ALU.mult, ALU.add).then_inc(q["acc_done"], 1)
                j = k - 8
                if b.has(j):
                    start_min(q, b, j, 1)
                j = k - 4
                if b.has(j):
                    masks(q, b, j, 1)
                j = k - 8
                if b.has(j):
                    dve.wait_ge(q["min_in_done"], b.count(j))
                    dve.wait_ge(q["scores_ready"], b.count(j))
                    apart(dve)
                    V.tensor_tensor_reduce(out=score_r[:, j % R, 0:G], in0=bank[(3, 7)[j % 2]][:, 0:G], in1=off_r[:, j % R, :],
                                           scale=1.0, scalar=min_in_r[:, j % R, 0:1], op0=ALU.add, op1=ALU.min,
                                           accum_out=min_r[:, j % R, 0:1]).then_inc(q["min_done"], 1)
                j = k - 5
                if b.has(j):
                    dve.wait_ge(q["gathered"][j % R], b.landed("gathered", j))
                    dve.wait_ge(q["rel_ready"], b.count(j))
                    V.tensor_tensor(val_r[:, j % R, :, 0:F], rows_r[:, j % R, :, 0:F],
                                    bank[0][:, 0:G].rearrange("p (c f) -> p c f", c=2), ALU.mult).then_inc(q["val_done"], 1)

            HOP_STEPS = 13
            with dve.Fori(0, HOPS) as hop:
                at = dve.snap(hop * HOP_STEPS)
                n = [0]

                def hdo(ins):
                    ins.then_inc(hop_step, 1)
                    n[0] += 1
                    dve.wait_ge(hop_step, at + n[0])

                tiles = dve.snap(hop * LB)
                for t in range(LB):
                    dve.wait_ge(left_ready, tiles + (t + 1))
                    k = min(4, NB - 4 * t)
                    V.tensor_scalar(wide[:, 4 * t * P:(4 * t + k) * P], bank[2 + t % 2][:, 0:k * P], -1.0, None, ALU.mult).then_inc(left_copied, 1)
                pipeline(dve, hop, hop_dve_step, uses[1])
                dve.wait_ge(state_in, dve.snap(hop * (NB * 16) + 2 * NB * 16))
                hdo(V.tensor_scalar(stat[0][:, :, 0:1], state[:, :, F:F + 1], 1e-30, None, ALU.max))
                hdo(V.tensor_scalar(stat[0][:, :, 1:2], state[:, :, F + 1:F + 2], 1.0, None, ALU.max))
                hdo(V.reciprocal(stat[1][:], stat[0][:]))
                hdo(V.tensor_tensor(stat[2][:, :, 0:1], stat[1][:, :, 0:1], stat[1][:, :, 1:2], ALU.mult))
                hdo(V.tensor_tensor(agg[:], state[:, :, 0:F], stat[2][:, :, 0:1].to_broadcast([P, NB, F]), ALU.mult))
                hdo(V.tensor_tensor(tmp[:], agg[:], agg[:], ALU.mult))
                hdo(V.reduce_sum(stat[0][:, :, 0], tmp[:], axis=AX))
                hdo(V.tensor_scalar(stat[1][:, :, 0:1], stat[0][:, :, 0:1], 1e-24, None, ALU.max))
                dve.sem_inc(var_ready, 1)
                dve.wait_ge(std_ready, hop + 4)
                hdo(V.reciprocal(stat[2][:, :, 1], stat[2][:, :, 0]))
                hdo(V.tensor_tensor(agg[:], agg[:], stat[2][:, :, 1:2].to_broadcast([P, NB, F]), ALU.mult))
                hdo(V.tensor_tensor(xs[:], xs[:], agg[:], ALU.add))
                hdo(V.memset(acc_r, 0.0))
                hdo(V.memset(min_r, 0.0))
                assert n[0] == HOP_STEPS
                dve.sem_inc(hop_done, 1)
                dve.sem_inc(agg_ready, 1)
            dve.sem_inc(out_ready, 1)


_INS = ["x", "src", "dst", "edge_type_64", "L0_gnn_W", "L0_gnn_attn_l", "L0_gnn_attn_r", "L0_gnn_bias", "L0_gnn_gamma",
        "L0_gnn_beta", "L1_gnn_edge_emb", "L1_gnn_q_w", "L1_gnn_k_w"]


def kernel(**inputs):
    import numpy as np
    import concourse.bacc as bacc
    from concourse.bass_utils import run_bass_kernel_spmd

    nc = bacc.Bacc("TRN2", target_bir_lowering=False, num_devices=1)
    arrays, args = {}, []
    for name in _INS:
        a = np.ascontiguousarray(inputs[name])
        arrays[f"in_{name}"] = a
        args.append(nc.dram_tensor(f"in_{name}", a.shape, mybir.dt.from_np(a.dtype), kind="ExternalInput").ap())
    result = nc.dram_tensor("out_x", (N, F), F32, kind="ExternalOutput").ap()
    gnn_kernel(nc, *args, result)
    r = run_bass_kernel_spmd(nc, [arrays], core_ids=[0])
    return r.results[0]["out_x"]
```

```python
from contextlib import ExitStack

import concourse.bass as bass
import concourse.mybir as mybir

P = 128
N = 6250
E = 206250
F = 128
NB = -(-N // P)
NLAST = N - (NB - 1) * P
HEADS = 2
FH = F // HEADS
RELS = 64
HOPS = 3
SLOPE = 0.2
EPS = 1e-5

G = 256
U = 14
R = 7
WINDOWS = -(-E // G)
BODIES = -(-(WINDOWS + NB - 1) // U)
NG = BODIES * U
COLS = -(-E // P)
LASTCOLS = E - (P - 1) * COLS
CH = 31
CHUNKS = COLS // (2 * CH)
EARLY_CHUNKS = 3
EARLY = EARLY_CHUNKS * 2 * CH
TILES = NG * G // P
LANES = TILES // U
WIDTH = U * P
SHIFT = 13
PADKEY = 7 << 10
MASK = (1 << SHIFT) - 1
NOWHERE = 2.0 * E
BIG = 1e30
ARENA = 10 * COLS
FB = -(-NB // 3)
LB = -(-NB // 4)
POOL_BLOCKS, ACT_BLOCKS = 25, 37
SW = F + 2
TW = 2 * (FH + 2)
MW = 4
KEEP, RESET, FORGET, TARGET = range(MW)
assert 2 * CH * CHUNKS == COLS and P * COLS == WINDOWS * G and N < MASK and RELS <= 64 and E * 64 + NB < 1 << 24

ALU = mybir.AluOpType
ACT = mybir.ActivationFunctionType
AX = mybir.AxisListType.X
F32 = mybir.dt.float32
BF16 = mybir.dt.bfloat16
I32 = mybir.dt.int32
U16 = mybir.dt.uint16


class Body:

    def __init__(self, eng, hop, i, uses):
        self.first = isinstance(i, int) and i == 0
        self.last = isinstance(i, int) and i == BODIES
        self.at = i * U if isinstance(i, int) else eng.snap(i * U)
        self.eng = eng

        def value(per_hop, per_body):
            v = i * per_body
            if hop is not None:
                v = v + hop * per_hop
            return v if isinstance(v, int) else eng.snap(v)

        self.groups = value(NG, U)
        self.used = {name: value(BODIES * (U // ring) * inc, (U // ring) * inc) for name, (ring, inc) in uses.items()}
        self.uses = uses

    def has(self, j):
        return (j >= 0 or not self.first) and (j < 0 or not self.last)

    def count(self, j):
        return self.groups + (j + 1)

    def landed(self, name, j):
        ring, inc = self.uses[name]
        return self.used[name] + inc * (j // ring + 1)


def pipeline(eng, hop, step, uses):
    b = Body(eng, hop, 0, uses)
    for k in range(U):
        step(b, k)
    with eng.Fori(1, BODIES) as i:
        b = Body(eng, hop, i, uses)
        for k in range(U):
            step(b, k)
    b = Body(eng, hop, BODIES, uses)
    for k in range(U):
        step(b, k)


def gnn_kernel(nc, x, src, dst, etype, w, attn_l, attn_r, bias, gamma, beta, emb, q_w, k_w, out):
    with ExitStack() as ctx:
        ctx.enter_context(nc.allow_non_contiguous_dma(reason="narrow columns of edges and scores"))

        def sb(name, shape, dt=F32):
            return ctx.enter_context(nc.sbuf_tensor(name, shape, dt))

        def sem(name):
            return ctx.enter_context(nc.semaphore(name))

        def dram(name, shape, dt):
            return nc.dram_tensor(name, shape, dt).ap()

        sorted_edges = [dram(f"sorted_edges{s}", ((WINDOWS + 1) * G, 1), I32) for s in range(2)]
        windows_d = [dram(f"windows{s}_d", (NG,), I32) for s in range(2)]
        key_d = [dram(f"key{s}_d", (NG * G,), U16) for s in range(2)]
        type_d = dram("type_d", (NG * G,), U16)
        meta_d = [dram(f"meta{s}_d", (P, NG, MW), F32) for s in range(2)]
        feat_d = dram("feat_d", (NB * P, TW), F32)
        er_d = dram("er_d", (NB, P, HEADS), F32)
        agg_d = dram("agg_d", (NB * P, F), F32)
        left_d = dram("left_d", (NB, F, P), F32)
        state_d = dram("state_d", (P, NG * SW), F32)

        xs = sb("xs", [P, NB, F])
        agg = sb("agg", [P, NB, F])
        tmp = sb("tmp", [P, NB, F])
        wide = sb("wide", [P, NB * TW])
        state = wide[:, 0:NB * SW].rearrange("p (b c) -> p b c", c=SW)
        feat = wide[:, 0:NB * TW].rearrange("p (b c) -> p b c", c=TW)
        left = wide[:, 0:NB * P].rearrange("p (b c) -> p b c", c=P)
        er = sb("er", [P, NB, HEADS])
        stat = [sb(f"stat{i}", [P, NB, 2]) for i in range(3)]

        ident = sb("ident", [P, P])
        ones = sb("ones", [P, P])
        before = sb("before", [P, P])
        rowid = sb("rowid", [P, P])
        giota = sb("giota", [P, NG])
        biota = sb("biota", [P, 64])
        w_s = sb("w_s", [P, F])
        wx = sb("wx", [P, TW + HEADS])
        junk = sb("junk", [P, FH])
        al_s = sb("al_s", [P, F])
        ar_s = sb("ar_s", [P, F])
        bias_s = sb("bias_s", [P, F])
        gamma_s = sb("gamma_s", [P, F])
        beta_s = sb("beta_s", [P, F])
        emb_s = sb("emb_s", [RELS, F])
        emb_rest = sb("emb_rest", [RELS, F])
        emb3 = sb("emb3", [RELS, 3, F], BF16)
        qw_s = sb("qw_s", [P, F])
        kw_s = sb("kw_s", [P, F])
        plan = [sb(f"plan{s}", [P, NG], I32) for s in range(2)]
        window_of = [sb(f"window_of{s}", [LANES, R], I32) for s in range(2)]
        peers = [sb(f"peers{s}", [P, TILES], I32) for s in range(2)]
        lastg = [sb(f"lastg{s}", [P, NB], I32) for s in range(2)]
        last_row = [sb(f"last_row{s}", [P, NB], I32) for s in range(2)]
        unsorted = sb("unsorted", [P, 1], I32)
        few = sb("few", [P, 16])
        counts = sb("counts", [P, NB])
        rows = [sb(f"rows{i}", [P, NB]) for i in range(8)]
        rowsi = [sb(f"rowsi{i}", [P, NB], I32) for i in range(2)]
        stage = sb("stage", [P, 2, 2, CH], I32)
        colid = sb("colid", [P, P])
        first_row = sb("first_row", [P, 1])
        offset_rows = sb("offset_rows", [NB, P])
        tmp_flat = tmp[:].rearrange("p b f -> p (b f)")
        tmp_meta = tmp_flat[:, 0:NG * MW]
        agg_flat = agg[:].rearrange("p b f -> p (b f)")
        scratch = [agg_flat[:, i * NG:(i + 1) * NG] for i in range(4)]
        member = agg_flat[:, 4 * NG:5 * NG]
        batchT = tmp_flat[:, 0:1024].rearrange("p (a b) -> p a b", a=2)

        arena = sb("arena", [P, ARENA])

        def column(i, dt=F32, cols=COLS, n=P, odd=0):
            a = arena[:, i * cols:(i + 1) * cols]
            return (a if dt is F32 else a.bitcast(dt))[0:n, odd * cols:(odd + 1) * cols]

        src_i, dst_i, type_i = column(0, I32), column(1, I32), column(2, I32)
        pos_f, run_f = column(3), column(4)
        pos_i = [column(5, I32), column(6, I32)]
        packed, spare_i = column(7, I32), column(8, I32)
        high = column(9, BF16)
        mask = column(9, U16, odd=1)
        shifted_i = column(5, I32)

        def lane_array(flat, i, dt=F32, odd=0):
            a = flat[:, i * WIDTH:(i + 1) * WIDTH]
            return (a if dt is F32 else a.bitcast(dt))[0:LANES, odd * WIDTH:(odd + 1) * WIDTH]

        s_packed, s_field, s_other = (lane_array(agg_flat, i, I32) for i in range(3))
        s_peer, s_part = lane_array(tmp_flat, 0), lane_array(tmp_flat, 1, I32)
        s_key, s_type16 = lane_array(tmp_flat, 2, U16), lane_array(tmp_flat, 2, U16, 1)
        sentinel = wide[0:1, 0:2 * G].bitcast(I32)
        spaces = {"arena": [arena[:], 0, ARENA], "agg": [agg_flat, 0, NB * F], "tmp": [tmp_flat, 1024, NB * F], "wide": [wide[:], 0, NB * TW]}

        def ring(shape, dt=F32, space="arena"):
            n = 1
            for d in shape:
                n *= d
            words = n if dt in (F32, I32) else -(-n // 2)
            flat, at, end = spaces[space]
            a = flat[:, at:at + words]
            spaces[space][1] += words
            assert at + words <= end, space
            if dt is not F32:
                a = a.bitcast(dt)
            if len(shape) == 2:
                return a.rearrange("p (a b) -> p a b", a=shape[0])
            return a.rearrange("p (a b c) -> p a b c", a=shape[0], b=shape[1])

        peer_r = ring((U, 2), I32)
        key_r = ring((U, G), U16, "wide")
        type_r = ring((U, G), U16, "wide")
        unit_meta = ring((U, MW))
        meta_r = ring((U, MW))
        er_r = ring((U, HEADS))
        left_r = ring((U, P), F32, "wide")
        rows_r = ring((R, 2, TW), F32, "agg")
        hot_r = ring((R, G), BF16)
        off_r = ring((R, G), BF16)
        val_r = ring((R, 2, F + 1))
        nohit_r = ring((R, G), BF16, "tmp")
        valT_r = ring((R, G), F32, "tmp")
        right_r = ring((R, G), F32, "tmp")
        cnt_r = ring((R, 1))
        min_in_r = ring((R, HEADS))
        fade_r = ring((R, HEADS))
        min_r = ring((R, HEADS))
        alpha_r = ring((R, HEADS))
        acc_r = ring((U, SW))
        relu_r = ring((2, HEADS * G))
        score_r = ring((R, HEADS * G), F32, "agg")
        prob_r = ring((2, HEADS * G))
        probT_r = ring((R, 2 * HEADS, P))

        bank = [ctx.enter_context(nc.psum_tensor(f"bank{i}", [P, 512], F32)) for i in range(8)]

        inputs_in = sem("inputs_in")
        edges_in = sem("edges_in")
        pads_set = sem("pads_set")
        consts_made = sem("consts_made")
        rowid_made = sem("rowid_made")
        dve_step = sem("dve_step")
        bucket_step = sem("bucket_step")
        early_step = sem("early_step")
        count_step = sem("count_step")
        hop_step = sem("hop_step")
        counts_ready = sem("counts_ready")
        totals_ready = sem("totals_ready")
        member_ready = sem("member_ready")
        blocks_ready = sem("blocks_ready")
        positions_ready = sem("positions_ready")
        meta_ready = sem("meta_ready")
        meta_stored = sem("meta_stored")
        staged = [[sem(f"staged{s}{i}") for i in range(2)] for s in range(2)]
        scattered = [[sem(f"scattered{s}{i}") for i in range(2)] for s in range(2)]
        resorted_in = sem("resorted_in")
        decoded = sem("decoded")
        sorted_stored = sem("sorted_stored")
        peerT_ready = sem("peerT_ready")
        peerT_copied = sem("peerT_copied")
        prefilled = sem("prefilled")
        packed_ready = sem("packed_ready")
        packed_stored = sem("packed_stored")
        order_counted = sem("order_counted")
        order_summed = sem("order_summed")
        order_known = sem("order_known")
        windows_stored = sem("windows_stored")
        windows_in = sem("windows_in")
        var_ready = sem("var_ready")
        std_ready = sem("std_ready")
        hidden_ready = sem("hidden_ready")
        hiddenT_ready = sem("hiddenT_ready")
        hiddenT_copied = sem("hiddenT_copied")
        feat_ready = sem("feat_ready")
        feat_copied = sem("feat_copied")
        feat_whole = sem("feat_whole")
        feat_stored = sem("feat_stored")
        weights_ready = sem("weights_ready")
        agg_ready = sem("agg_ready")
        aggT_ready = sem("aggT_ready")
        aggT_copied = sem("aggT_copied")
        left_ready = sem("left_ready")
        left_copied = sem("left_copied")
        hop_stored = sem("hop_stored")
        state_in = sem("state_in")
        state_gathered = sem("state_gathered")
        hop_done = sem("hop_done")
        out_ready = sem("out_ready")
        out_stored = sem("out_stored")
        passed = {e.engine: sem(f"passed{i}") for i, e in enumerate((nc.vector, nc.gpsimd, nc.sync, nc.scalar))}
        pipes_free = sem("pipes_free")
        pipes = []
        for q in ("attn_", "hop_"):
            pipes.append({
                "unit": [sem(f"{q}unit_loaded{i}") for i in range(2)],
                "block": [sem(f"{q}block_loaded{i}") for i in range(U)],
                "gathered": [sem(f"{q}gathered{i}") for i in range(R)],
                "stored": [sem(f"{q}stored{i}") for i in range(2)],
                **{n: sem(q + n) for n in (
                    "off_done", "min_in_done", "scores_ready", "relu_done", "neg_done", "min_done", "exp_done",
                    "probT_ready", "probT_copied", "sum_ready", "acc_done", "rel_ready", "val_done", "valT_ready",
                    "valT_copied", "right_ready", "right_done",
                    "fade_done")},
            })
        block = ctx.enter_context(nc.Block())

        def apart(eng):
            eng.sem_inc(passed[eng.engine], 1)

        uses = [{"unit": (U, 48), "block": (U, 16), "gathered": (R, 32), "stored": (U, 16)},
                {"unit": (U, 64), "block": (U, 16), "gathered": (R, 32), "stored": (U, 16)}]
        STORE = [10, 13]

        @block.sync
        def _(sp):
            sp.wait_ge(pads_set, 1)
            for a, d in ((src_i, src), (dst_i, dst), (type_i, etype)):
                sp.dma_start(a[0:P - 1, :], d[0:(P - 1) * COLS].rearrange("(p c) -> p c", p=P - 1)).then_inc(edges_in, 16)
                sp.dma_start(a[P - 1:P, 0:LASTCOLS], d[(P - 1) * COLS:E].rearrange("(p c) -> p c", p=1)).then_inc(edges_in, 16)
            sp.dma_start(shifted_i[0:P - 1, :], dst[1:(P - 1) * COLS + 1].rearrange("(p c) -> p c", p=P - 1)).then_inc(edges_in, 16)
            sp.dma_start(shifted_i[P - 1:P, 0:LASTCOLS - 1], dst[(P - 1) * COLS + 1:E].rearrange("(p c) -> p c", p=1)).then_inc(edges_in, 16)
            for s in range(2):
                first = (WINDOWS - s) * G
                sp.dma_start(sorted_edges[s][first:].rearrange("(l w) o -> l (w o)", l=1), sentinel[:, 0:(s + 1) * G]).then_inc(prefilled, 16)
            sp.dma_start(xs[:, 0:NB - 1, :], x[0:(NB - 1) * P, :].rearrange("(b p) f -> p b f", p=P)).then_inc(inputs_in, 16)
            sp.dma_start(xs[0:NLAST, NB - 1, :], x[(NB - 1) * P:N, :]).then_inc(inputs_in, 16)
            for a, d in ((w_s, w), (qw_s, q_w), (kw_s, k_w), (emb_s, emb)):
                sp.dma_start(a[:], d).then_inc(inputs_in, 16)
            for a, d in ((al_s, attn_l.rearrange("a b -> (a b)")), (ar_s, attn_r.rearrange("a b -> (a b)")), (bias_s, bias), (gamma_s, gamma), (beta_s, beta)):
                sp.dma_start(a[:], d.partition_broadcast(P)).then_inc(inputs_in, 16)

            sp.wait_ge(packed_ready, 1)
            sp.dma_start(sorted_edges[0][0:P * COLS].rearrange("(p c) o -> p (c o)", p=P), packed).then_inc(packed_stored, 16)

            def stage_all(s):
                def stage_chunk(i, h, first):
                    if not first:
                        sp.wait_ge(scattered[s][h], sp.snap(i * (16 * CH)))
                        apart(sp)
                    at = i * (2 * CH) + h * CH
                    sp.dma_start(stage[:, h, 0, :], pos_i[s][:, bass.ds(at, CH)]).then_inc(staged[s][h], 16)
                    sp.dma_start(stage[:, h, 1, :], packed[:, bass.ds(at, CH)]).then_inc(staged[s][h], 16)

                for h in range(2):
                    stage_chunk(0, h, True)
                with sp.Fori(1, EARLY_CHUNKS) as i:
                    for h in range(2):
                        stage_chunk(i, h, False)
                if s == 1:
                    sp.wait_ge(positions_ready, 2)
                    apart(sp)
                with sp.Fori(EARLY_CHUNKS, CHUNKS) as i:
                    for h in range(2):
                        stage_chunk(i, h, False)
                for h in range(2):
                    sp.wait_ge(scattered[s][h], CHUNKS * 16 * CH)

            sp.wait_ge(positions_ready, 1)
            stage_all(1)
            sp.wait_ge(positions_ready, 3)
            sp.wait_ge(order_known, 1)
            n = sp.value_load(unsorted[0:1, 0:1], min_val=0, max_val=E)
            with sp.If(n > 0):
                stage_all(0)
            with sp.Else():
                apart(sp)
            for s in range(2):
                sp.wait_ge(decoded, s + 1)
                sp.dma_start(key_d[s].rearrange("(l w) -> l w", l=LANES), s_key).then_inc(sorted_stored, 16)
                if s == 1:
                    sp.dma_start(type_d.rearrange("(l w) -> l w", l=LANES), s_type16).then_inc(sorted_stored, 16)
            sp.wait_ge(meta_stored, 32)
            sp.wait_ge(sorted_stored, 3 * 16)
            sp.wait_ge(pipes_free, 1)

            def load_store(layer):
                q = pipes[layer]

                def step(b, k):
                    j = k
                    if not b.last and k % R == 0:
                        if not b.first:
                            sp.wait_ge(q["off_done"], b.count(j - R - 1))
                            apart(sp)
                            sp.wait_ge(q["gathered"][(j - R - 1) % R], b.landed("gathered", j - R - 1))
                            apart(sp)
                        g = b.at + k
                        d = q["unit"][j // R]
                        at = (lambda a, n: a[:, g * n:(g + R) * n] if b.first else a[:, bass.ds(g * n, R * n)])
                        row = (lambda a: a[g * G:(g + R) * G] if b.first else a[bass.ds(g * G, R * G)])
                        flat = (lambda a: a[:, k:k + R, :].rearrange("p a b -> p (a b)"))
                        sp.dma_start(flat(peer_r), at(peers[layer], 2)).then_inc(d, 16)
                        sp.dma_start(flat(key_r), row(key_d[layer]).partition_broadcast(P)).then_inc(d, 16)
                        sp.dma_start(flat(unit_meta), at(meta_d[layer].rearrange("p g c -> p (g c)"), MW)).then_inc(d, 16)
                        if layer == 1:
                            sp.dma_start(flat(type_r)[0:RELS], row(type_d).partition_broadcast(RELS)).then_inc(d, 16)
                    if not b.last:
                        if not b.first:
                            sp.wait_ge(q["relu_done" if layer == 0 else "scores_ready"], b.count(j - U))
                            apart(sp)
                        g = b.at + k
                        blk = sp.value_load(plan[layer][0:1, g:g + 1] if b.first else plan[layer][0:1, bass.ds(g, 1)],
                                            min_val=0, max_val=NB - 1)
                        if layer == 0:
                            sp.dma_start(er_r[:, j % U, :], er_d[bass.ds(blk, 1)].rearrange("o p c -> p (o c)")).then_inc(q["block"][j % U], 16)
                        else:
                            sp.dma_start(left_r[:, j % U, :], left_d[bass.ds(blk, 1)].rearrange("o f n -> f (o n)")).then_inc(q["block"][j % U], 16)
                    j = k - STORE[layer]
                    if b.has(j) and j % R == R - 1:
                        sp.wait_ge(q["acc_done"], b.count(j))
                        apart(sp)
                        g = b.at + (j - R + 1)
                        to = state_d[:, g * SW:(g + R) * SW] if isinstance(g, int) else state_d[:, bass.ds(g * SW, R * SW)]
                        sp.dma_start(to, acc_r[:, (j - R + 1) % U:j % U + 1, :].rearrange("p a b -> p (a b)")).then_inc(q["stored"][(j // R) % 2], 16)
                return step

            def load_states(layer):
                apart(sp)
                with sp.Fori(POOL_BLOCKS, ACT_BLOCKS) as b:
                    g = sp.value_load(lastg[layer][0:1, bass.ds(b, 1)], min_val=0, max_val=NG - 1)
                    sp.dma_start(wide[:, bass.ds(b * SW, SW)], state_d[:, bass.ds(g * SW, SW)]).then_inc(state_in, 16)

            pipeline(sp, None, load_store(0), uses[0])
            for i in range(2):
                sp.wait_ge(pipes[0]["stored"][i], 16 * BODIES)
            load_states(0)

            with sp.Fori(0, HOPS) as hop:
                sp.wait_ge(agg_ready, hop + 1)
                sp.dma_start(agg_d.rearrange("(b p) f -> p b f", p=P), agg[:]).then_inc(hop_stored, 16)
                sp.wait_ge(left_copied, sp.snap(hop * LB + LB))
                sp.dma_start(left_d.rearrange("b f n -> f b n"), left).then_inc(hop_stored, 16)
                sp.wait_ge(hop_stored, sp.snap(hop * 32 + 32))
                pipeline(sp, hop, load_store(1), uses[1])
                for i in range(2):
                    sp.wait_ge(pipes[1]["stored"][i], sp.snap(hop * (16 * BODIES) + 16 * BODIES))
                load_states(1)
                sp.wait_ge(hop_done, hop + 1)
                apart(sp)
            sp.wait_ge(out_ready, 1)
            sp.dma_start(out[0:(NB - 1) * P, :].rearrange("(b p) f -> p b f", p=P), xs[:, 0:NB - 1, :]).then_inc(out_stored, 16)
            sp.dma_start(out[(NB - 1) * P:N, :], xs[0:NLAST, NB - 1, :]).then_inc(out_stored, 16)
            sp.wait_ge(out_stored, 32)

        @block.gpsimd
        def _(pool):
            nc.gpsimd.iota(giota[:], [[1, NG]], base=0, channel_multiplier=0, allow_small_or_imprecise_dtypes=True)
            nc.gpsimd.iota(biota[:], [[1, 64]], base=0, channel_multiplier=0, allow_small_or_imprecise_dtypes=True)
            nc.gpsimd.iota(rowid[:], [[0, P]], base=0, channel_multiplier=1, allow_small_or_imprecise_dtypes=True)
            nc.gpsimd.iota(colid[:], [[1, P]], base=0, channel_multiplier=0, allow_small_or_imprecise_dtypes=True).then_inc(rowid_made, 1)

            pool.wait_ge(prefilled, 32)
            pool.wait_ge(packed_stored, 16)
            def scatter_all(s):
                with pool.Fori(0, CHUNKS) as i:
                    for h in range(2):
                        pool.wait_ge(staged[s][h], pool.snap(i * 32 + 32))
                        apart(pool)
                        for c in range(CH):
                            nc.gpsimd.indirect_dma_start(
                                out=sorted_edges[s], out_offset=bass.IndirectOffsetOnAxis(ap=stage[:, h, 0, c:c + 1], axis=0),
                                in_=stage[:, h, 1, c:c + 1], in_offset=None, bounds_check=WINDOWS * G - 1, oob_is_err=False,
                            ).then_inc(scattered[s][h], 16)

            scatter_all(1)
            pool.wait_ge(order_known, 1)
            n = pool.value_load(unsorted[0:1, 0:1], min_val=0, max_val=E)
            with pool.If(n > 0):
                scatter_all(0)
                for h in range(2):
                    pool.wait_ge(scattered[0][h], CHUNKS * 16 * CH)
                apart(pool)
            with pool.Else():
                apart(pool)
            for h in range(2):
                pool.wait_ge(scattered[1][h], CHUNKS * 16 * CH)
            for s in range(2):
                if s == 0:
                    pool.wait_ge(windows_in, 32)
                    pool.wait_ge(feat_stored, 32)
                else:
                    pool.wait_ge(decoded, 1)
                apart(pool)
                for k in range(R):
                    nc.gpsimd.indirect_dma_start(
                        out=s_packed[:, k * G:(k + 1) * G], out_offset=None, in_=sorted_edges[s].rearrange("(w e) o -> w (e o)", e=G),
                        in_offset=bass.IndirectOffsetOnAxis(ap=window_of[s][:, k:k + 1], axis=0)).then_inc(resorted_in, 16)

            def gather(layer):
                q = pipes[layer]
                table = (feat_d, agg_d)[layer]
                width = (TW, F)[layer]

                def step(b, k):
                    if b.last:
                        return
                    pool.wait_ge(q["unit"][k // R], b.landed("unit", k))
                    if not (b.first and k < R):
                        pool.wait_ge(q["sum_ready" if layer == 0 else "val_done"], b.count(k - R))
                    apart(pool)
                    for c in range(2):
                        nc.gpsimd.indirect_dma_start(
                            out=rows_r[:, k % R, c, 0:width], out_offset=None, in_=table,
                            in_offset=bass.IndirectOffsetOnAxis(ap=peer_r[:, k, c:c + 1], axis=0),
                        ).then_inc(q["gathered"][k % R], 16)
                return step

            def gather_states(layer, h):
                for i in range(2):
                    pool.wait_ge(pipes[layer]["stored"][i], 16 * BODIES if h is None else pool.snap(h * (16 * BODIES) + 16 * BODIES))
                apart(pool)
                for b in range(POOL_BLOCKS):
                    nc.gpsimd.indirect_dma_start(
                        out=wide[:, b * SW:(b + 1) * SW], out_offset=None, in_=state_d.rearrange("p (g c) -> (p g) c", c=SW),
                        in_offset=bass.IndirectOffsetOnAxis(ap=last_row[layer][:, b:b + 1], axis=0)).then_inc(state_gathered, 16)

            pool.wait_ge(feat_stored, 32)
            pool.wait_ge(pipes_free, 1)
            pipeline(pool, None, gather(0), uses[0])
            gather_states(0, None)
            with pool.Fori(0, HOPS) as hop:
                pool.wait_ge(hop_stored, pool.snap(hop * 32 + 32))
                apart(pool)
                pipeline(pool, hop, gather(1), uses[1])
                gather_states(1, hop)

        @block.tensor
        def _(pe):
            def mm(out, lhsT, rhs, start=True, stop=True):
                return nc.tensor.matmul(out, lhsT, rhs, start=start, stop=stop)

            pe.wait_ge(consts_made, 1)
            pe.wait_ge(order_counted, 1)
            mm(bank[3][:, 0:1], ones[:], few[:, 9:10]).then_inc(order_summed, 1)
            for o, s in enumerate((1, 0)):
                pe.wait_ge(counts_ready, o + 1)
                mm(bank[0][:, 0:NB], before[:], counts[:])
                mm(bank[1][:, 0:NB], ones[:], counts[:]).then_inc(totals_ready, 1)
                pe.wait_ge(member_ready, o + 1)
                for i, table in enumerate((rowid[0:NB, :], offset_rows[:])):
                    for h in range(2):
                        last = mm(bank[3 + 2 * i + h][:, 0:NG // 2], table, member[0:NB, h * (NG // 2):(h + 1) * (NG // 2)])
                last.then_inc(blocks_ready, 1)

            pe.wait_ge(hidden_ready, 1)
            pe.wait_ge(weights_ready, 1)
            for t in range(FB + 1):
                if t < FB:
                    if t >= 2:
                        pe.wait_ge(hiddenT_copied, t - 1)
                    for i in range(min(3, NB - 3 * t)):
                        last = nc.tensor.transpose(bank[t % 2][:, i * P:(i + 1) * P], agg[:, 3 * t + i, :], ident[:])
                    last.then_inc(hiddenT_ready, 1)
                if t >= 1:
                    pe.wait_ge(hiddenT_copied, t)
                    if t >= 3:
                        pe.wait_ge(feat_copied, t - 2)
                    for i in range(min(3, NB - 3 * (t - 1))):
                        last = mm(bank[2 + (t - 1) % 2][:, i * (TW + HEADS):(i + 1) * (TW + HEADS)],
                                  batchT[:, (t - 1) % 2, i * P:(i + 1) * P], wx[:])
                    last.then_inc(feat_ready, 1)

            for s in range(2):
                for t in range(U):
                    if t == 0:
                        pe.wait_ge(decoded, s + 1)
                    if s * U + t >= 4:
                        pe.wait_ge(peerT_copied, s * U + t - 3)
                    nc.tensor.transpose(bank[4 + t % 4 if s == 0 else 4 + (t + U) % 4][:, 0:LANES], s_peer[:, t * P:(t + 1) * P],
                                        ident[0:LANES, 0:LANES]).then_inc(peerT_ready, 1)
            q = pipes[0]

            def attn_step(b, k):
                j = k - 5
                if b.has(j):
                    pe.wait_ge(q["gathered"][j % R], b.landed("gathered", j))
                    if not (b.first and j < 2):
                        pe.wait_ge(q["neg_done"], b.count(j - 2))
                    elif b.first and j == 0:
                        pe.wait_ge(feat_whole, 1)
                    for h in range(HEADS):
                        for c in range(2):
                            last = nc.tensor.transpose(
                                bank[j % 2][:, h * G + c * P:h * G + (c + 1) * P],
                                rows_r[:, j % R, c, h * (FH + 2) + FH + 1:h * (FH + 2) + FH + 2].to_broadcast([P, P]), ident[:])
                    last.then_inc(q["scores_ready"], 1)
                j = k - 7
                if b.has(j):
                    pe.wait_ge(q["exp_done"], b.count(j))
                    for i in range(2 * HEADS):
                        last = nc.tensor.transpose(bank[2 + j % 2][:, i * P:(i + 1) * P], prob_r[:, j % 2, i * P:(i + 1) * P], ident[:])
                    last.then_inc(q["probT_ready"], 1)
                j = k - 8
                if b.has(j):
                    if not (b.first and j < 2):
                        pe.wait_ge(q["acc_done"], b.count(j - 2))
                    pe.wait_ge(q["probT_copied"], b.count(j))
                    for h in range(HEADS):
                        for c in range(2):
                            last = mm(bank[4 + j % 2][:, h * (FH + 1):(h + 1) * (FH + 1)], probT_r[:, j % R, 2 * h + c, :],
                                      rows_r[:, j % R, c, h * (FH + 2):h * (FH + 2) + FH + 1], c == 0, c == 1)
                    last.then_inc(q["sum_ready"], 1)

            pipeline(pe, None, attn_step, uses[0])

            h_ = pipes[1]

            def hop_pe_step(b, k):
                q = h_
                j = k - 11
                if b.has(j):
                    if not (b.first and j < 2):
                        pe.wait_ge(q["acc_done"], b.count(j - 2))
                    pe.wait_ge(q["probT_copied"], b.count(j))
                    for c in range(2):
                        last = mm(bank[5 + j % 2][:, 0:F + 1], probT_r[:, j % R, c, :], val_r[:, j % R, c, :], c == 0, c == 1)
                    last.then_inc(q["sum_ready"], 1)
                j = k - 10
                if b.has(j):
                    pe.wait_ge(q["exp_done"], b.count(j))
                    for c in range(2):
                        last = nc.tensor.transpose(bank[4][:, c * P:(c + 1) * P], prob_r[:, j % 2, c * P:(c + 1) * P], ident[:])
                    last.then_inc(q["probT_ready"], 1)
                j = k - 8
                if b.has(j):
                    pe.wait_ge(q["block"][j % U], b.landed("block", j))
                    pe.wait_ge(q["right_done"], b.count(j))
                    mm(bank[(3, 7)[j % 2]][:, 0:G], left_r[:, j % U, :], right_r[:, j % R, :]).then_inc(q["scores_ready"], 1)
                j = k - 7
                if b.has(j):
                    pe.wait_ge(q["valT_copied"], b.count(j))
                    mm(bank[2][:, 0:G], kw_s[:], valT_r[:, j % R, :]).then_inc(q["right_ready"], 1)
                j = k - 6
                if b.has(j):
                    pe.wait_ge(q["val_done"], b.count(j))
                    for c in range(2):
                        last = nc.tensor.transpose(bank[1][:, c * P:(c + 1) * P], val_r[:, j % R, c, 0:F], ident[:])
                    last.then_inc(q["valT_ready"], 1)
                j = k - 5
                if b.has(j):
                    pe.wait_ge(q["off_done"], b.count(j))
                    for c in range(2):
                        for i in range(3):
                            last = mm(bank[0][:, c * P:(c + 1) * P], hot_r[0:RELS, j % R, c * P:(c + 1) * P], emb3[:, i, :], i == 0, i == 2)
                    last.then_inc(q["rel_ready"], 1)

            with pe.Fori(0, HOPS) as hop:
                pe.wait_ge(agg_ready, hop + 1)
                tiles = pe.snap(hop * LB)
                for t in range(LB + 1):
                    if t < LB:
                        if t >= 2:
                            pe.wait_ge(aggT_copied, tiles + (t - 1))
                        for i in range(min(4, NB - 4 * t)):
                            last = nc.tensor.transpose(bank[t % 2][:, i * P:(i + 1) * P], agg[:, 4 * t + i, :], ident[:])
                        last.then_inc(aggT_ready, 1)
                    if t >= 1:
                        pe.wait_ge(aggT_copied, tiles + t)
                        if t >= 3:
                            pe.wait_ge(left_copied, tiles + (t - 2))
                        n = min(4, NB - 4 * (t - 1)) * P
                        mm(bank[2 + (t - 1) % 2][:, 0:n], qw_s[:], batchT[:, (t - 1) % 2, 0:n]).then_inc(left_ready, 1)
                pe.wait_ge(left_copied, tiles + LB)
                pipeline(pe, hop, hop_pe_step, uses[1])

        @block.scalar
        def _(act):
            def root(n):
                act.wait_ge(var_ready, n)
                nc.scalar.activation(stat[2][:, :, 0:1], stat[1][:, :, 0:1], ACT.Sqrt).then_inc(std_ready, 1)

            for o, s in enumerate((1, 0)):
                act.wait_ge(meta_ready, o + 1)
                act.dma_start(windows_d[s].rearrange("(a g) -> a g", a=1), plan[s][32:33, :]).then_inc(windows_stored, 16)
                act.dma_start(meta_d[s].rearrange("p g c -> p (g c)"), (tmp_meta, wide[:, 0:NG * MW])[s]).then_inc(meta_stored, 16)
                act.wait_ge(windows_stored, (o + 1) * 16)
                act.dma_start(window_of[s][:], windows_d[s].rearrange("(l k) -> l k", k=R)).then_inc(windows_in, 16)
            root(1)
            for t in range(FB):
                act.wait_ge(hiddenT_ready, t + 1)
                if t >= 2:
                    act.wait_ge(feat_ready, t - 1)
                n = min(3, NB - 3 * t) * P
                nc.scalar.copy(batchT[:, t % 2, 0:n], bank[t % 2][:, 0:n]).then_inc(hiddenT_copied, 1)
            act.wait_ge(feat_whole, 1)
            act.dma_start(feat_d.rearrange("(b p) c -> p b c", p=P), feat).then_inc(feat_stored, 16)
            act.dma_start(er_d.rearrange("b p h -> p b h"), er[:]).then_inc(feat_stored, 16)
            def load_states(layer, h):
                for i in range(2):
                    act.wait_ge(pipes[layer]["stored"][i], 16 * BODIES if h is None else act.snap(h * (16 * BODIES) + 16 * BODIES))
                apart(act)
                with act.Fori(ACT_BLOCKS, NB) as b:
                    g = act.value_load(lastg[layer][0:1, bass.ds(b, 1)], min_val=0, max_val=NG - 1)
                    act.dma_start(wide[:, bass.ds(b * SW, SW)], state_d[:, bass.ds(g * SW, SW)]).then_inc(state_in, 16)

            q = pipes[0]

            def attn_step(b, k):
                j = k - 7
                if b.has(j):
                    act.wait_ge(q["min_done"], b.count(j))
                    for h in range(HEADS):
                        last = nc.scalar.activation(prob_r[:, j % 2, h * G:(h + 1) * G], score_r[:, j % R, h * G:(h + 1) * G],
                                                    ACT.Exp, scale=-1.0, bias=min_r[:, j % R, h:h + 1])
                    last.then_inc(q["exp_done"], 1)
                j = k - 5
                if b.has(j):
                    act.wait_ge(q["block"][j % U], b.landed("block", j))
                    act.wait_ge(q["scores_ready"], b.count(j))
                    for h in range(HEADS):
                        last = nc.scalar.activation(relu_r[:, j % 2, h * G:(h + 1) * G], bank[j % 2][:, h * G:(h + 1) * G],
                                                    ACT.Relu, scale=1.0 - SLOPE, bias=er_r[:, j % U, h:h + 1])
                    last.then_inc(q["relu_done"], 1)
                j = k - 7
                if b.has(j):
                    act.wait_ge(q["fade_done"], b.count(j))
                    nc.scalar.activation(alpha_r[:, j % R, :], fade_r[:, j % R, :], ACT.Exp, bias=meta_r[:, j % U, FORGET:FORGET + 1])
                    act.wait_ge(q["probT_ready"], b.count(j))
                    nc.scalar.copy(probT_r[:, j % R, :, :], bank[2 + j % 2][:].rearrange("p (a b) -> p a b", b=P)).then_inc(q["probT_copied"], 1)

            pipeline(act, None, attn_step, uses[0])
            load_states(0, None)
            root(2)
            root(3)
            h_ = pipes[1]

            def hop_act_step(b, k):
                q = h_
                j = k - 9
                if b.has(j):
                    act.wait_ge(q["min_done"], b.count(j))
                    nc.scalar.activation(prob_r[:, j % 2, 0:G], score_r[:, j % R, 0:G], ACT.Exp, scale=-1.0,
                                         bias=min_r[:, j % R, 0:1]).then_inc(q["exp_done"], 1)
                    nc.scalar.activation(nohit_r[:, j % R, :], off_r[:, j % R, :], ACT.Exp, scale=-1.0, accum_out=cnt_r[:, j % R, 0:1])
                    act.wait_ge(q["fade_done"], b.count(j))
                    nc.scalar.activation(alpha_r[:, j % R, 0:1], fade_r[:, j % R, 0:1], ACT.Exp, bias=meta_r[:, j % U, FORGET:FORGET + 1])
                j = k - 10
                if b.has(j):
                    act.wait_ge(q["probT_ready"], b.count(j))
                    nc.scalar.copy(probT_r[:, j % R, 0:2, :], bank[4][:, 0:G].rearrange("p (a b) -> p a b", b=P)).then_inc(q["probT_copied"], 1)
                j = k - 7
                if b.has(j):
                    act.wait_ge(q["right_ready"], b.count(j))
                    nc.scalar.activation(right_r[:, j % R, :], bank[2][:, 0:G], ACT.Tanh).then_inc(q["right_done"], 1)
                j = k - 6
                if b.has(j):
                    act.wait_ge(q["valT_ready"], b.count(j))
                    nc.scalar.copy(valT_r[:, j % R, :], bank[1][:, 0:G]).then_inc(q["valT_copied"], 1)

            with act.Fori(0, HOPS) as hop:
                tiles = act.snap(hop * LB)
                for t in range(LB):
                    act.wait_ge(aggT_ready, tiles + (t + 1))
                    if t >= 2:
                        act.wait_ge(left_ready, tiles + (t - 1))
                    n = min(4, NB - 4 * t) * P
                    nc.scalar.copy(batchT[:, t % 2, 0:n], bank[t % 2][:, 0:n]).then_inc(aggT_copied, 1)
                pipeline(act, hop, hop_act_step, uses[1])
                load_states(1, hop)
                act.wait_ge(var_ready, hop + 4)
                nc.scalar.activation(stat[2][:, :, 0:1], stat[1][:, :, 0:1], ACT.Sqrt).then_inc(std_ready, 1)

        @block.vector
        def _(dve):
            V = nc.vector
            steps = [0]

            def do(ins):
                ins.then_inc(dve_step, 1)
                steps[0] += 1
                dve.wait_ge(dve_step, steps[0])

            def signal(s):
                dve.sem_inc(s, 1)

            for a in (src_i, dst_i, type_i):
                V.memset(a, PADKEY)
            V.memset(shifted_i, PADKEY)
            V.memset(sentinel, PADKEY << SHIFT | PADKEY)
            V.memset(xs[:], 0.0)
            V.memset(wx[:], 0.0).then_inc(pads_set, 1)
            do(V.memset(ones[:], 1.0))
            dve.wait_ge(rowid_made, 1)
            V.tensor_scalar(first_row[:], rowid[:, 0:1], float(NG), None, ALU.mult)
            V.tensor_tensor(ident[:], rowid[:], colid[:], ALU.is_equal)
            V.tensor_tensor(before[:], rowid[:], colid[:], ALU.is_lt).then_inc(consts_made, 1)
            dve.wait_ge(edges_in, 8 * 16)
            do(V.tensor_tensor(run_f, shifted_i, dst_i, ALU.is_lt))
            do(V.reduce_sum(few[:, 9:10], run_f, axis=AX))
            signal(order_counted)
            do(V.tensor_scalar(spare_i, type_i, 2 * SHIFT, None, ALU.logical_shift_left))
            do(V.tensor_scalar(packed, dst_i, SHIFT, None, ALU.logical_shift_left))
            do(V.tensor_tensor(spare_i, spare_i, packed, ALU.bitwise_or))
            do(V.tensor_tensor(packed, spare_i, src_i, ALU.bitwise_or))
            signal(packed_ready)
            dve.wait_ge(order_summed, 1)
            do(V.tensor_copy(unsorted[:], bank[3][:, 0:1]))
            signal(order_known)

            signal(count_step)
            signal(bucket_step)
            signal(early_step)

            def find_positions(o, s):
                key = (dst_i, src_i)[s]
                do(V.tensor_scalar(spare_i, key, 7, None, ALU.logical_shift_right))
                do(V.tensor_copy(high, spare_i))
                with dve.Fori(0, NB) as b:
                    n = dve.snap(b + (o * NB + 1))
                    dve.wait_ge(count_step, n)
                    V.tensor_scalar(mask.bitcast(BF16), high, biota[:, bass.ds(b, 1)], None, ALU.is_equal, ALU.add,
                                    accum_out=counts[:, bass.ds(b, 1)]).then_inc(count_step, 1)
                dve.wait_ge(count_step, (o + 1) * NB + 1)
                signal(counts_ready)
                dve.wait_ge(totals_ready, o + 1)
                upto_last, before_first, last_window, first_window, n_groups, end, start, lane_start = (r[:] for r in rows)
                do(V.tensor_tensor_scan(upto_last, ones[:, 0:NB], bank[1][:, 0:NB], 0.0, ALU.mult, ALU.add))
                do(V.tensor_tensor(before_first, upto_last, bank[1][:, 0:NB], ALU.subtract))
                for edges, windows, more in ((upto_last, last_window, G - 1), (before_first, first_window, 0)):
                    do(V.tensor_scalar(rowsi[0][:], edges, float(more), None, ALU.add))
                    do(V.tensor_scalar(rowsi[1][:], rowsi[0][:], G.bit_length() - 1, None, ALU.logical_shift_right))
                    do(V.tensor_copy(windows, rowsi[1][:]))
                do(V.tensor_tensor(n_groups, last_window, first_window, ALU.subtract))
                do(V.tensor_scalar(n_groups, n_groups, 1.0, None, ALU.max))
                do(V.tensor_tensor_scan(end, ones[:, 0:NB], n_groups, 0.0, ALU.mult, ALU.add))
                do(V.tensor_tensor(start, end, n_groups, ALU.subtract))
                do(V.tensor_tensor(first_window, first_window, start, ALU.subtract))
                do(V.tensor_scalar(lastg[s][:], end, -1.0, None, ALU.add))
                do(V.tensor_scalar(upto_last, end, 1.0, first_row[:, 0:1], ALU.subtract, ALU.add))
                do(V.tensor_copy(last_row[s][:], upto_last))
                do(V.tensor_tensor(lane_start, before_first, bank[0][:, 0:NB], ALU.add))
                for c, r in ((0, start), (1, end), (2, first_window)):
                    do(V.tensor_tensor(upto_last[0:NB], r[0:NB], ident[0:NB, 0:NB], ALU.mult))
                    do(V.reduce_sum(few[0:NB, c:c + 1], upto_last[0:NB], axis=AX))
                do(V.tensor_scalar(few[0:NB, 3:4], rowid[0:NB, 0:1], float(NB - 1), 1e6, ALU.is_equal, ALU.mult))
                do(V.tensor_tensor(few[0:NB, 4:5], few[0:NB, 3:4], few[0:NB, 1:2], ALU.add))
                do(V.tensor_scalar(scratch[0][0:NB, :], giota[0:NB, :], few[0:NB, 0:1], None, ALU.is_ge))
                do(V.scalar_tensor_tensor(member[0:NB, :], giota[0:NB, :], few[0:NB, 4:5], scratch[0][0:NB, :], ALU.is_lt, ALU.mult))
                do(V.tensor_scalar(offset_rows[:], ones[0:NB, :], few[0:NB, 2:3], None, ALU.mult))
                signal(member_ready)
                dve.wait_ge(blocks_ready, o + 1)
                half_g = NG // 2
                for h in range(2):
                    c = slice(h * half_g, (h + 1) * half_g)
                    do(V.tensor_copy(scratch[1][:, c], bank[3 + h][:, 0:half_g]))
                    do(V.tensor_tensor(scratch[2][:, c], giota[:, c], bank[5 + h][:, 0:half_g], ALU.add))
                do(V.tensor_copy(plan[s][0:1, :], scratch[1][0:1, :]))
                do(V.tensor_scalar(plan[s][32:33, :], scratch[2][32:33, :], float(WINDOWS), None, ALU.min))
                meta = (tmp_meta, wide[:, 0:NG * MW])[s].rearrange("p (g c) -> p g c", c=MW)
                m = [meta[:, :, i] for i in range(MW)]
                if o == 0:
                    dve.wait_ge(prefilled, 32)
                do(V.memset(m[KEEP], 0.0))
                do(V.tensor_tensor(m[KEEP][:, 1:NG], scratch[1][:, 1:NG], scratch[1][:, 0:NG - 1], ALU.is_equal))
                do(V.tensor_scalar(m[RESET], m[KEEP], -0.5 * BIG, 0.5 * BIG, ALU.mult, ALU.add))
                do(V.tensor_scalar(m[FORGET], m[KEEP], 0.25 * BIG, -0.25 * BIG, ALU.mult, ALU.add))
                do(V.tensor_scalar(m[TARGET], scratch[1], float(P), rowid[:, 0:1], ALU.mult, ALU.add))
                signal(meta_ready)
                do(V.memset(pos_f, NOWHERE))
                if s == 1:
                    c = slice(0, EARLY)
                    with dve.Fori(0, NB) as b:
                        n = dve.snap(b * 4 + 1)
                        dve.wait_ge(early_step, n)
                        V.tensor_scalar(mask[:, c], high[:, c], biota[:, bass.ds(b, 1)], None, ALU.is_equal).then_inc(early_step, 1)
                        dve.wait_ge(early_step, n + 1)
                        V.tensor_tensor_scan(run_f[:, c], ones[:, 0:1].to_broadcast([P, EARLY]), mask[:, c], rows[7][:, bass.ds(b, 1)],
                                             ALU.mult, ALU.add).then_inc(early_step, 1)
                        dve.wait_ge(early_step, n + 2)
                        apart(dve)
                        V.tensor_copy(rows[7][:, bass.ds(b, 1)], run_f[:, EARLY - 1:EARLY]).then_inc(early_step, 1)
                        V.copy_predicated(pos_f[:, c], mask[:, c], run_f[:, c]).then_inc(early_step, 1)
                    dve.wait_ge(early_step, 4 * NB + 1)
                    do(V.tensor_scalar(pos_i[s][:, c], pos_f[:, c], -1.0, None, ALU.add))
                    signal(positions_ready)
                c = slice(EARLY if s == 1 else 0, COLS)
                with dve.Fori(0, NB) as b:
                    n = dve.snap(b * 3 + (o * 3 * NB + 1))
                    dve.wait_ge(bucket_step, n)
                    V.tensor_scalar(mask[:, c], high[:, c], biota[:, bass.ds(b, 1)], None, ALU.is_equal).then_inc(bucket_step, 1)
                    dve.wait_ge(bucket_step, n + 1)
                    V.tensor_tensor_scan(run_f[:, c], ones[:, 0:1].to_broadcast([P, COLS - c.start]), mask[:, c], rows[7][:, bass.ds(b, 1)],
                                         ALU.mult, ALU.add).then_inc(bucket_step, 1)
                    dve.wait_ge(bucket_step, n + 2)
                    apart(dve)
                    V.copy_predicated(pos_f[:, c], mask[:, c], run_f[:, c]).then_inc(bucket_step, 1)
                dve.wait_ge(bucket_step, (o + 1) * 3 * NB + 1)
                do(V.tensor_scalar(pos_i[s][:, c], pos_f[:, c], -1.0, None, ALU.add))
                signal(positions_ready)

            find_positions(0, 1)
            find_positions(1, 0)

            def norm(src_t, dst_t, n):
                do(V.reduce_sum(stat[0][:, :, 0], src_t, axis=AX))
                do(V.tensor_scalar(stat[0][:, :, 1], stat[0][:, :, 0], 1.0 / F, None, ALU.mult))
                do(V.tensor_tensor(tmp[:], src_t, stat[0][:, :, 1:2].to_broadcast([P, NB, F]), ALU.subtract))
                do(V.tensor_tensor(dst_t, tmp[:], tmp[:], ALU.mult))
                do(V.reduce_sum(stat[1][:, :, 1], dst_t, axis=AX))
                do(V.tensor_scalar(stat[1][:, :, 0], stat[1][:, :, 1], 1.0 / F, EPS, ALU.mult, ALU.add))
                signal(var_ready)
                dve.wait_ge(std_ready, n)
                do(V.reciprocal(stat[2][:, :, 1], stat[2][:, :, 0]))
                do(V.tensor_tensor(dst_t, tmp[:], stat[2][:, :, 1:2].to_broadcast([P, NB, F]), ALU.mult))

            dve.wait_ge(inputs_in, 11 * 16)
            for h in range(HEADS):
                c0 = h * (FH + 2)
                do(V.tensor_copy(wx[:, c0:c0 + FH], w_s[:, h * FH:(h + 1) * FH]))
                do(V.tensor_tensor(junk[:], w_s[:, h * FH:(h + 1) * FH], al_s[:, h * FH:(h + 1) * FH], ALU.mult))
                do(V.reduce_sum(wx[:, c0 + FH + 1:c0 + FH + 2], junk[:], axis=AX))
                do(V.tensor_tensor(junk[:], w_s[:, h * FH:(h + 1) * FH], ar_s[:, h * FH:(h + 1) * FH], ALU.mult))
                do(V.reduce_sum(wx[:, TW + h:TW + h + 1], junk[:], axis=AX))
            do(V.tensor_copy(emb3[:, 0, :], emb_s[:]))
            do(V.tensor_tensor(emb_rest[:], emb_s[:], emb3[:, 0, :], ALU.subtract))
            do(V.tensor_copy(emb3[:, 1, :], emb_rest[:]))
            do(V.tensor_tensor(emb_s[:], emb_rest[:], emb3[:, 1, :], ALU.subtract))
            do(V.tensor_copy(emb3[:, 2, :], emb_s[:]))
            signal(weights_ready)

            dve.wait_ge(meta_stored, 32)
            norm(xs[:], agg[:], 1)
            do(V.tensor_scalar(agg[:], agg[:], 0.0, None, ALU.max))
            signal(hidden_ready)
            for t in range(FB):
                dve.wait_ge(feat_ready, t + 1)
                k = min(3, NB - 3 * t)
                s_ = bank[2 + t % 2][:, 0:k * (TW + HEADS)].rearrange("p (b c) -> p b c", b=k)
                V.tensor_copy(feat[:, 3 * t:3 * t + k, :], s_[:, :, 0:TW])
                V.tensor_scalar(er[:, 3 * t:3 * t + k, :], s_[:, :, TW:TW + HEADS], 1.0 - SLOPE, None, ALU.mult).then_inc(feat_copied, 1)
            dve.wait_ge(feat_copied, FB)
            for h in range(HEADS):
                do(V.memset(feat[:, :, h * (FH + 2) + FH:h * (FH + 2) + FH + 1], 1.0))
            signal(feat_whole)

            for s in range(2):
                dve.wait_ge(resorted_in, (s + 1) * 16 * R)
                if s == 1:
                    dve.wait_ge(sorted_stored, 16)
                do(V.tensor_scalar(s_field, s_packed, MASK, None, ALU.bitwise_and))
                do(V.tensor_scalar(s_part, s_packed, SHIFT, None, ALU.logical_shift_right))
                do(V.tensor_scalar(s_other, s_part, MASK, None, ALU.bitwise_and))
                do(V.tensor_copy(s_key, (s_other, s_field)[s]))
                do(V.tensor_scalar(s_peer, (s_field, s_other)[s], float(N - 1), None, ALU.min))
                if s == 1:
                    do(V.tensor_scalar(s_part, s_packed, 2 * SHIFT, None, ALU.logical_shift_right))
                    do(V.tensor_copy(s_type16, s_part))
                signal(decoded)
                by_lane = peers[s][:].rearrange("p (l t) -> p l t", t=U)
                for t in range(U):
                    dve.wait_ge(peerT_ready, s * U + t + 1)
                    V.tensor_copy(by_lane[:, :, t], bank[4 + (s * U + t) % 4][:, 0:LANES]).then_inc(peerT_copied, 1)
                dve.wait_ge(peerT_copied, (s + 1) * U)
            dve.wait_ge(sorted_stored, 3 * 16)
            do(V.memset(acc_r, 0.0))
            do(V.memset(min_r, 0.0))
            signal(pipes_free)
            dve.wait_ge(feat_stored, 32)

            q0 = pipes[0]

            def masks(q, b, j, layer):
                dve.wait_ge(q["unit"][(j // R) % 2], b.landed("unit", j))
                if j % R == 0:
                    at = j % U
                    if not (b.first and j < U):
                        dve.wait_ge(q["acc_done"], b.count(j - R - 1))
                    V.tensor_copy(meta_r[:, at:at + R, :], unit_meta[:, at:at + R, :])
                if layer == 1:
                    V.tensor_scalar(hot_r[0:RELS, j % R, :], type_r[0:RELS, j % U, :], rowid[0:RELS, 0:1], None, ALU.is_equal)
                V.tensor_scalar(off_r[:, j % R, :], key_r[:, j % U, :], unit_meta[:, j % U, TARGET:TARGET + 1], BIG,
                                ALU.not_equal, ALU.mult).then_inc(q["off_done"], 1)

            def start_min(q, b, j, n):
                m = meta_r[:, j % U, :]
                dve.wait_ge(q["off_done"], b.count(j))
                if not (b.first and j == 0):
                    dve.wait_ge(q["min_done"], b.count(j - 1))
                V.tensor_scalar(min_in_r[:, j % R, 0:n], min_r[:, (j - 1) % R, 0:n], m[:, KEEP:KEEP + 1], m[:, RESET:RESET + 1],
                                ALU.mult, ALU.add).then_inc(q["min_in_done"], 1)

            def fade(q, b, j, n):
                dve.wait_ge(q["min_done"], b.count(j))
                V.tensor_tensor(fade_r[:, j % R, 0:n], min_r[:, j % R, 0:n], min_in_r[:, j % R, 0:n], ALU.subtract).then_inc(q["fade_done"], 1)

            def accumulate(q, b, j):
                dve.wait_ge(q["sum_ready"], b.count(j))
                if not (b.first and j == 0):
                    dve.wait_ge(q["acc_done"], b.count(j - 1))
                if j % R == 0 and not (b.first and j < U):
                    dve.wait_ge(q["stored"][(j // R) % 2], b.landed("stored", j - U))

            def attn_step(b, k):
                q = q0
                j = k - 9
                if b.has(j):
                    accumulate(q, b, j)
                    for h in range(HEADS):
                        c = slice(h * (FH + 1), (h + 1) * (FH + 1))
                        last = V.scalar_tensor_tensor(acc_r[:, j % U, c], acc_r[:, (j - 1) % U, c], alpha_r[:, j % R, h:h + 1],
                                                      bank[4 + j % 2][:, c], ALU.mult, ALU.add)
                    last.then_inc(q["acc_done"], 1)
                j = k - 7
                if b.has(j):
                    fade(q, b, j, HEADS)
                j = k - 6
                if b.has(j):
                    start_min(q, b, j, HEADS)
                    dve.wait_ge(q["relu_done"], b.count(j))
                    V.scalar_tensor_tensor(score_r[:, j % R, :], bank[j % 2][:], -SLOPE, relu_r[:, j % 2, :], ALU.mult, ALU.subtract).then_inc(q["neg_done"], 1)
                j = k - 4
                if b.has(j):
                    masks(q, b, j, 0)
                j = k - 6
                if b.has(j):
                    dve.wait_ge(q["min_in_done"], b.count(j))
                    dve.wait_ge(q["neg_done"], b.count(j))
                    apart(dve)
                    for h in range(HEADS):
                        last = V.tensor_tensor_reduce(out=score_r[:, j % R, h * G:(h + 1) * G], in0=score_r[:, j % R, h * G:(h + 1) * G],
                                                      in1=off_r[:, j % R, :], scale=1.0, scalar=min_in_r[:, j % R, h:h + 1],
                                                      op0=ALU.add, op1=ALU.min, accum_out=min_r[:, j % R, h:h + 1])
                    last.then_inc(q["min_done"], 1)

            pipeline(dve, None, attn_step, uses[0])

            dve.wait_ge(state_in, (NB - POOL_BLOCKS) * 16)
            dve.wait_ge(state_gathered, POOL_BLOCKS * 16)
            st = state.rearrange("p b (h c) -> p b h c", h=HEADS)
            do(V.tensor_scalar(stat[0][:], st[:, :, :, FH], 1e-30, None, ALU.max))
            do(V.reciprocal(stat[1][:], stat[0][:]))
            for h in range(HEADS):
                do(V.tensor_tensor(agg[:, :, h * FH:(h + 1) * FH], st[:, :, h, 0:FH], stat[1][:, :, h:h + 1].to_broadcast([P, NB, FH]), ALU.mult))
            every = lambda a: a[:].rearrange("p (o f) -> p o f", o=1).to_broadcast([P, NB, F])
            do(V.tensor_tensor(agg[:], agg[:], every(bias_s), ALU.add))
            norm(agg[:], agg[:], 2)
            do(V.tensor_tensor(agg[:], agg[:], every(gamma_s), ALU.mult))
            do(V.tensor_tensor(agg[:], agg[:], every(beta_s), ALU.add))
            do(V.tensor_tensor(xs[:], xs[:], agg[:], ALU.add))
            norm(xs[:], agg[:], 3)
            do(V.tensor_scalar(agg[:], agg[:], 0.0, None, ALU.max))
            do(V.scalar_tensor_tensor(xs[:], agg[:], float(HOPS), xs[:], ALU.mult, ALU.add))
            do(V.memset(val_r, 1.0))
            do(V.memset(acc_r, 0.0))
            signal(agg_ready)
            q1 = pipes[1]

            def hop_dve_step(b, k):
                q = q1
                j = k - 12
                if b.has(j):
                    accumulate(q, b, j)
                    V.tensor_scalar(acc_r[:, j % U, F + 1:F + 2], acc_r[:, (j - 1) % U, F + 1:F + 2], meta_r[:, j % U, KEEP:KEEP + 1],
                                    cnt_r[:, j % R, 0:1], ALU.mult, ALU.add)
                    V.scalar_tensor_tensor(acc_r[:, j % U, 0:F + 1], acc_r[:, (j - 1) % U, 0:F + 1], alpha_r[:, j % R, 0:1],
                                           bank[5 + j % 2][:, 0:F + 1], ALU.mult, ALU.add).then_inc(q["acc_done"], 1)
                j = k - 9
                if b.has(j):
                    fade(q, b, j, 1)
                j = k - 8
                if b.has(j):
                    start_min(q, b, j, 1)
                j = k - 4
                if b.has(j):
                    masks(q, b, j, 1)
                j = k - 8
                if b.has(j):
                    dve.wait_ge(q["min_in_done"], b.count(j))
                    dve.wait_ge(q["scores_ready"], b.count(j))
                    apart(dve)
                    V.tensor_tensor_reduce(out=score_r[:, j % R, 0:G], in0=bank[(3, 7)[j % 2]][:, 0:G], in1=off_r[:, j % R, :],
                                           scale=1.0, scalar=min_in_r[:, j % R, 0:1], op0=ALU.add, op1=ALU.min,
                                           accum_out=min_r[:, j % R, 0:1]).then_inc(q["min_done"], 1)
                j = k - 5
                if b.has(j):
                    dve.wait_ge(q["gathered"][j % R], b.landed("gathered", j))
                    dve.wait_ge(q["rel_ready"], b.count(j))
                    V.tensor_tensor(val_r[:, j % R, :, 0:F], rows_r[:, j % R, :, 0:F],
                                    bank[0][:, 0:G].rearrange("p (c f) -> p c f", c=2), ALU.mult).then_inc(q["val_done"], 1)

            HOP_STEPS = 13
            with dve.Fori(0, HOPS) as hop:
                at = dve.snap(hop * HOP_STEPS)
                n = [0]

                def hdo(ins):
                    ins.then_inc(hop_step, 1)
                    n[0] += 1
                    dve.wait_ge(hop_step, at + n[0])

                tiles = dve.snap(hop * LB)
                for t in range(LB):
                    dve.wait_ge(left_ready, tiles + (t + 1))
                    k = min(4, NB - 4 * t)
                    V.tensor_scalar(wide[:, 4 * t * P:(4 * t + k) * P], bank[2 + t % 2][:, 0:k * P], -1.0, None, ALU.mult).then_inc(left_copied, 1)
                pipeline(dve, hop, hop_dve_step, uses[1])
                n_loads = (NB - POOL_BLOCKS) * 16
                dve.wait_ge(state_in, dve.snap(hop * n_loads + 2 * n_loads))
                dve.wait_ge(state_gathered, dve.snap(hop * (POOL_BLOCKS * 16) + 2 * POOL_BLOCKS * 16))
                hdo(V.tensor_scalar(stat[0][:, :, 0:1], state[:, :, F:F + 1], 1e-30, None, ALU.max))
                hdo(V.tensor_scalar(stat[0][:, :, 1:2], state[:, :, F + 1:F + 2], 1.0, None, ALU.max))
                hdo(V.reciprocal(stat[1][:], stat[0][:]))
                hdo(V.tensor_tensor(stat[2][:, :, 0:1], stat[1][:, :, 0:1], stat[1][:, :, 1:2], ALU.mult))
                hdo(V.tensor_tensor(agg[:], state[:, :, 0:F], stat[2][:, :, 0:1].to_broadcast([P, NB, F]), ALU.mult))
                hdo(V.tensor_tensor(tmp[:], agg[:], agg[:], ALU.mult))
                hdo(V.reduce_sum(stat[0][:, :, 0], tmp[:], axis=AX))
                hdo(V.tensor_scalar(stat[1][:, :, 0:1], stat[0][:, :, 0:1], 1e-24, None, ALU.max))
                dve.sem_inc(var_ready, 1)
                dve.wait_ge(std_ready, hop + 4)
                hdo(V.reciprocal(stat[2][:, :, 1], stat[2][:, :, 0]))
                hdo(V.tensor_tensor(agg[:], agg[:], stat[2][:, :, 1:2].to_broadcast([P, NB, F]), ALU.mult))
                hdo(V.tensor_tensor(xs[:], xs[:], agg[:], ALU.add))
                hdo(V.memset(acc_r, 0.0))
                hdo(V.memset(min_r, 0.0))
                assert n[0] == HOP_STEPS
                dve.sem_inc(hop_done, 1)
                dve.sem_inc(agg_ready, 1)
            dve.sem_inc(out_ready, 1)


_INS = ["x", "src", "dst", "edge_type_64", "L0_gnn_W", "L0_gnn_attn_l", "L0_gnn_attn_r", "L0_gnn_bias", "L0_gnn_gamma",
        "L0_gnn_beta", "L1_gnn_edge_emb", "L1_gnn_q_w", "L1_gnn_k_w"]


def kernel(**inputs):
    import numpy as np
    import concourse.bacc as bacc
    from concourse.bass_utils import run_bass_kernel_spmd

    nc = bacc.Bacc("TRN2", target_bir_lowering=False, num_devices=1)
    arrays, args = {}, []
    for name in _INS:
        a = np.ascontiguousarray(inputs[name])
        arrays[f"in_{name}"] = a
        args.append(nc.dram_tensor(f"in_{name}", a.shape, mybir.dt.from_np(a.dtype), kind="ExternalInput").ap())
    result = nc.dram_tensor("out_x", (N, F), F32, kind="ExternalOutput").ap()
    gnn_kernel(nc, *args, result)
    r = run_bass_kernel_spmd(nc, [arrays], core_ids=[0])
    return r.results[0]["out_x"]
```
